# Optimizing a Trainium2 kernel written in Bass

```python
import numpy as np
import jax
import jax.numpy as jnp

def _softmax(x, axis=-1):
    return jax.nn.softmax(x, axis=axis)

def _gelu(x):
    return jax.nn.gelu(x, approximate=True)

def _silu(x):
    return jax.nn.silu(x)

def _sigmoid(x):
    return jax.nn.sigmoid(x)

def _layernorm(x, axis=-1, eps=1e-05):
    m = jnp.mean(x, axis=axis, keepdims=True)
    v = jnp.var(x, axis=axis, keepdims=True)
    return (x - m) / jnp.sqrt(v + eps)

def _scatter_add(tgt, idx, src, axis=0):
    return tgt.at[idx].add(src)

def _segment_sum(src, seg, n):
    return jax.ops.segment_sum(src, seg, n)
kernel_name = 'mk_xattn_ffn_d1_seqx_r2_69805d'

def setup_inputs(seed: int=0):
    np.random.seed(seed)
    _w = jnp.asarray

    def _rec_inputs():
        import jax
        import jax.numpy as jnp
        _rk = jax.random.key(seed)
        x = -0.0005207 + 1.001 * jax.random.normal(jax.random.fold_in(_rk, 1), (128, 256, 512), jnp.float32)
        _lenS = 256 - jax.random.randint(jax.random.fold_in(_rk, 7), (128,), 0, max(1, 256 // 4) + 1, jnp.int32)
        _lenS2 = 256 - jax.random.randint(jax.random.fold_in(_rk, 8), (128,), 0, max(1, 256 // 4) + 1, jnp.int32)
        _ctx_1024P = jax.random.normal(jax.random.fold_in(_rk, 11), (128, 16, 512), jnp.float32)
        _ctx_1024c = jax.random.dirichlet(jax.random.fold_in(_rk, 511), 0.3 * jnp.ones((16,), jnp.float32), (128, 256))
        _ctx_1024t = jnp.einsum('bsk,bkd->bsd', _ctx_1024c, _ctx_1024P)
        _ctx_1024t = _ctx_1024t * jax.lax.rsqrt(jnp.mean(jnp.square(_ctx_1024t)) + 1e-12) * 0.953939
        ctx_1024 = -0.000514642 + 1.00011 * (_ctx_1024t + 0.3 * jax.random.normal(jax.random.fold_in(_rk, 611), (128, 256, 512), jnp.float32))
        return (x, ctx_1024)
    x, ctx_1024 = _rec_inputs()

    def _L0_xattn_setup():
        import jax, jax.numpy as jnp
        import numpy as np
        B, S, E, NH = (1, 1024, 512, 8)
        DH = E // NH
        EPS = 1e-06
        LN_EPS = 1e-05
        key = jax.random.key(seed)
        ks = jax.random.split(key, 8)
        q = jax.random.normal(ks[0], (B, S, E), dtype=jnp.float32)
        k = jax.random.normal(ks[1], (B, S, E), dtype=jnp.float32)
        v = jax.random.normal(ks[2], (B, S, E), dtype=jnp.float32)
        scale = 1.0 / np.sqrt(3 * E)
        igate_w = jax.random.normal(ks[3], (NH, 3 * E), dtype=jnp.float32) * scale
        igate_b = jax.random.normal(ks[4], (NH,), dtype=jnp.float32) * 0.1
        fgate_w = jax.random.normal(ks[5], (NH, 3 * E), dtype=jnp.float32) * scale
        fgate_b = jnp.linspace(3.0, 6.0, NH, dtype=jnp.float32)
        out_w = 1.0 + 0.1 * jax.random.normal(ks[6], (E,), dtype=jnp.float32)
        return {'q': q, 'k': k, 'v': v, 'igate_w': igate_w, 'igate_b': igate_b, 'fgate_w': fgate_w, 'fgate_b': fgate_b, 'out_w': out_w}
    _L0_xattn_all = _L0_xattn_setup()
    _L0_xattn_in = {k: v for k, v in _L0_xattn_all.items() if k in ('igate_w', 'igate_b', 'fgate_w', 'fgate_b', 'out_w')}
    del _L0_xattn_all

    def _L0_ffn_setup():
        import jax, jax.numpy as jnp
        import numpy as np
        FEATURES = 512
        D_IN = 512

        def fp8_gemm_optimized(x, input_scale, kernel, kernel_scale):
            s_in = input_scale[0]
            s_k = kernel_scale[0]
            x_q = (x.astype(jnp.float32) / s_in).astype(jnp.float8_e4m3fn)
            k_q = (kernel.astype(jnp.float32) / s_k).astype(jnp.float8_e4m3fn)
            y = jnp.dot(x_q.astype(jnp.float32), k_q.astype(jnp.float32), preferred_element_type=jnp.float32)
            return y * (s_in * s_k)
        key = jax.random.key(seed)
        kx, kk, kb = jax.random.split(key, 3)
        x = jax.random.normal(kx, (4, 4096, D_IN), dtype=jnp.float32)
        limit = np.sqrt(6.0 / (D_IN + FEATURES)).astype(np.float32)
        kernel = jax.random.uniform(kk, (D_IN, FEATURES), dtype=jnp.float32, minval=-limit, maxval=limit).astype(jnp.bfloat16)
        input_scale = jnp.ones((1,), dtype=jnp.float32)
        kernel_scale = jnp.ones((1,), dtype=jnp.float32)
        bias = jnp.zeros((FEATURES,), dtype=jnp.bfloat16)
        return {'x': x, 'kernel': kernel, 'input_scale': input_scale, 'kernel_scale': kernel_scale, 'bias': bias}
    _L0_ffn_all = _L0_ffn_setup()
    _L0_ffn_in = {k: v for k, v in _L0_ffn_all.items() if k in ('kernel', 'input_scale', 'kernel_scale', 'bias')}
    del _L0_ffn_all
    return {'x': x, 'ctx_1024': ctx_1024, 'L0_xattn_igate_w': _L0_xattn_in['igate_w'], 'L0_xattn_igate_b': _L0_xattn_in['igate_b'], 'L0_xattn_fgate_w': _L0_xattn_in['fgate_w'], 'L0_xattn_fgate_b': _L0_xattn_in['fgate_b'], 'L0_xattn_out_w': _L0_xattn_in['out_w'], 'L0_ffn_kernel': _L0_ffn_in['kernel'], 'L0_ffn_input_scale': _L0_ffn_in['input_scale'], 'L0_ffn_kernel_scale': _L0_ffn_in['kernel_scale'], 'L0_ffn_bias': _L0_ffn_in['bias']}

def reference(x, ctx_1024, L0_xattn_igate_w, L0_xattn_igate_b, L0_xattn_fgate_w, L0_xattn_fgate_b, L0_xattn_out_w, L0_ffn_kernel, L0_ffn_input_scale, L0_ffn_kernel_scale, L0_ffn_bias):
    import jax
    import jax.numpy as jnp

    def _L0_xattn_ref(q, k, v, igate_w, igate_b, fgate_w, fgate_b, out_w):
        import jax, jax.numpy as jnp
        import numpy as np
        B, S, E, NH = (1, 1024, 512, 8)
        DH = E // NH
        EPS = 1e-06
        LN_EPS = 1e-05
        Bq, Sq, Eq = q.shape
        nh = igate_b.shape[0]
        dh = Eq // nh
        gi = jnp.concatenate([q, k, v], axis=-1)
        ig = (gi @ igate_w.T + igate_b).transpose(0, 2, 1)
        fg = (gi @ fgate_w.T + fgate_b).transpose(0, 2, 1)
        qh = q.reshape(Bq, Sq, nh, dh).transpose(0, 2, 1, 3)
        kh = k.reshape(Bq, Sq, nh, dh).transpose(0, 2, 1, 3)
        vh = v.reshape(Bq, Sq, nh, dh).transpose(0, 2, 1, 3)
        log_f = jax.nn.log_sigmoid(fg)
        cs = jnp.cumsum(log_f, axis=-1)
        diff = cs[..., :, None] - cs[..., None, :]
        mask = jnp.tril(jnp.ones((Sq, Sq), dtype=bool))
        log_fg_mat = jnp.where(mask, diff, -jnp.inf)
        log_D = log_fg_mat + ig[..., None, :]
        max_log_D = jnp.max(log_D, axis=-1, keepdims=True)
        D = jnp.exp(log_D - max_log_D)
        qk = jnp.einsum('bhsd,bhtd->bhst', qh, kh) / jnp.sqrt(jnp.float32(dh))
        C = qk * D
        normalizer = jnp.maximum(jnp.abs(C.sum(-1, keepdims=True)), jnp.exp(-max_log_D))
        h = jnp.einsum('bhst,bhtd->bhsd', C / (normalizer + EPS), vh)
        mean = h.mean(-1, keepdims=True)
        var = ((h - mean) ** 2).mean(-1, keepdims=True)
        hn = (h - mean) / jnp.sqrt(var + LN_EPS)
        hn = hn * out_w.reshape(nh, dh)[None, :, None, :]
        return hn.transpose(0, 2, 1, 3).reshape(Bq, Sq, Eq)

    def _L0_ffn_ref(x, kernel, input_scale, kernel_scale, bias):
        import jax, jax.numpy as jnp
        import numpy as np
        FEATURES = 512
        D_IN = 512

        def fp8_gemm_optimized(x, input_scale, kernel, kernel_scale):
            s_in = input_scale[0]
            s_k = kernel_scale[0]
            x_q = (x.astype(jnp.float32) / s_in).astype(jnp.float8_e4m3fn)
            k_q = (kernel.astype(jnp.float32) / s_k).astype(jnp.float8_e4m3fn)
            y = jnp.dot(x_q.astype(jnp.float32), k_q.astype(jnp.float32), preferred_element_type=jnp.float32)
            return y * (s_in * s_k)
        dtype = jnp.bfloat16
        x = x.astype(dtype)
        orig_shape = x.shape
        x2 = x.reshape(-1, x.shape[-1])
        y = fp8_gemm_optimized(x2, input_scale, kernel, kernel_scale)
        y = y.astype(dtype) + bias
        return y.reshape(orig_shape[:-1] + (FEATURES,))
    x = x + _L0_xattn_ref(_layernorm(x, axis=-1), ctx_1024, ctx_1024, L0_xattn_igate_w, L0_xattn_igate_b, L0_xattn_fgate_w, L0_xattn_fgate_b, L0_xattn_out_w)
    x = x + _L0_ffn_ref(_layernorm(x, axis=-1), L0_ffn_kernel, L0_ffn_input_scale, L0_ffn_kernel_scale, L0_ffn_bias)
    return x

_drawn_inputs = setup_inputs


def setup_inputs(seed=0):
    import zlib

    import numpy as np

    out = dict(_drawn_inputs(seed))
    spreads = {'L0_ffn_bias': (0.0, 0.1)}
    factors = {'L0_xattn_igate_b': 64.0}
    for name, (base, spread) in spreads.items():
        noise = np.random.default_rng([zlib.crc32(name.encode()), seed]).standard_normal(out[name].shape)
        drawn = base * np.exp(spread * noise) if base else spread * noise
        out[name] = jnp.asarray(drawn.astype(out[name].dtype))
    for name, factor in factors.items():
        out[name] = (out[name] * factor).astype(out[name].dtype)
    return out
```

```python
from contextlib import ExitStack

import concourse.bass as bass
from concourse import mybir

P = 128
GROUP = 4
RING = 8


class Batch:

    def __init__(self, it, k):
        self.it, self.k = it, k

    def __add__(self, d):
        return Batch(self.it, self.k + d)

    def __sub__(self, d):
        return Batch(self.it, self.k - d)

    @property
    def known(self):
        return isinstance(self.it, int)

    @property
    def index(self):
        return self.it * RING + self.k

    def exists(self, batches):
        return not self.known or 0 <= self.index < batches

    def follows(self, batches):
        return not self.known or self.index >= batches

    def count(self, each, done, unit=1):
        return self.it * (each * RING // unit) + each * (self.k // unit) + done


class Stage:

    def __init__(self, sem, steps, unit=1):
        self.sem, self.steps, self.unit = sem, steps.split(), unit

    def at(self, batch, step):
        return batch.count(len(self.steps), self.steps.index(step) + 1, self.unit)


def build_kernel(nc, x, ctx, igate_w, igate_b, fgate_w, fgate_b, out_w, ffn_w, s_in, s_k, bias,
                 c_ident, c_gsel, c_hsel, out):
    f32, bf16, fp8, i32 = mybir.dt.float32, mybir.dt.bfloat16, mybir.dt.float8e4, mybir.dt.int32
    ALU, ACT, AX = mybir.AluOpType, mybir.ActivationFunctionType, mybir.AxisListType
    B, S, E = x.shape
    NH = igate_b.shape[0]
    DH = E // NH
    T = S // P
    C = E // P
    F = ffn_w.shape[1]
    R = GROUP * NH
    U = 2
    W = DH + 1
    EPS, LN_EPS = 1e-6, 1e-5
    Q_SCALE = DH ** -0.5
    TOP = 1e37
    assert (T, C, U, DH) == (2, 4, 2, 64) and B % RING == 0 and B >= 3 * RING

    es = ExitStack()
    with es:
        def sb(name, shape, dt=f32):
            return es.enter_context(nc.sbuf_tensor(name, shape, dt))

        def sem(name):
            return es.enter_context(nc.semaphore(name))

        x_sb = sb("x_sb", [P, RING, T, E])
        c_sb = sb("c_sb", [P, RING, T, E])
        qT = sb("qT", [P, RING, C, S])
        kT = sb("kT", [P, RING, C, S])
        val = sb("val", [P, 2, T * NH, W])
        g_sb = sb("g_sb", [P, 2, T * NH, W])
        x1 = sb("x1", [P, 2, T, E])
        q_nat = sb("q_nat", [P, T, E])
        bn1 = sb("bn1", [P, T, 6])
        mv1 = sb("mv1", [P, T, 2])
        log1 = sb("log1", [P, T])
        r1 = sb("r1", [P, T])
        r1q = sb("r1q", [P, T])
        nb1 = sb("nb1", [P, T])
        g_part = sb("g_part", [P, GROUP, S])
        z_abs = sb("z_abs", [R, S])
        ncs = sb("ncs", [R, S])
        am = sb("am", [R, 2 * S])
        mx = sb("mx", [R, S])
        ex = sb("ex", [R, 2 * S])
        z_f, z_neg = ex[:, 0:S], ex[:, S:2 * S]
        rest = sb("rest", [R, 2 * S])
        part2 = sb("part2", [R, 2 * S], bf16)
        split = sb("split", [3 * R, 2, 2 * S], bf16)
        facs = sb("facs", [P, 2, 4, R])
        v_sum = sb("v_sum", [P, T * NH])
        v_mean = sb("v_mean", [P, T * NH])
        k_w = sb("k_w", [P, E])
        dec = sb("dec", [P, 4, 4 * P])
        state = sb("state", [P, U, 2, 2 * W])
        carry = sb("carry", [P, NH, W])
        g_ss = sb("g_ss", [P, T * NH])
        h_n0 = sb("h_n0", [P, T, NH])
        h_n = sb("h_n", [P, T, NH])
        h_n1 = sb("h_n1", [P, T * NH])
        h_n2 = sb("h_n2", [P, T * NH])
        h_v = sb("h_v", [P, T * NH])
        h_vc = sb("h_vc", [P, T * NH])
        h_log = sb("h_log", [P, T * NH])
        h_r = sb("h_r", [P, T * NH])
        bn2 = sb("bn2", [P, T, 6])
        mv2 = sb("mv2", [P, T, 2])
        log2 = sb("log2", [P, T])
        r2 = sb("r2", [P, T])
        nb2 = sb("nb2", [P, T])
        z_bf = sb("z_bf", [P, T, E], bf16)
        zq = sb("zq", [P, C, S], fp8)
        y_bf = sb("y_bf", [P, T, F], bf16)
        o_sb = sb("o_sb", [P, T, F])
        ident = sb("ident", [P, P])
        ident_bf = sb("ident_bf", [P, P], bf16)
        gsel = sb("gsel", [P, GROUP, 2 * R])
        hsel_f = sb("hsel_f", [3 * R, R])
        hsel = sb("hsel", [3 * R, R], bf16)
        w_x = sb("w_x", [P, C, 32])
        w_c = sb("w_c", [P, C, 32])
        b_i = sb("b_i", [R, 1])
        b_f = sb("b_f", [R, 1])
        w_out = sb("w_out", [P, E])
        w_ffn = sb("w_ffn", [P, C, F], bf16)
        b_ffn = sb("b_ffn", [P, F], bf16)
        sc = sb("sc", [P, 2])
        s_inv = sb("s_inv", [P, 2])
        s_out = sb("s_out", [P, 1])
        ln_eps = sb("ln_eps", [P, 1])
        w_rows = x1[0:2 * NH, :, :, :].rearrange("p a t e -> p (a t e)")[:, 0:3 * E]
        f_val, f_mag, f_tmp = (dec[:, i, :] for i in range(3))

        bank = [es.enter_context(nc.psum_tensor(f"bank{i}", [P, 512], f32)) for i in range(8)]
        turn_ps = bank[0:2]
        gate_ps, arg_ps, qk_ps = bank[2], bank[3], bank[4]
        work_ps = bank[5:7]
        y_ps = bank[7]
        part_ps = gate_ps[:, 0:S]
        rows_ps = gate_ps[0:2 * R, S:2 * S]
        facs_ps = gate_ps[:, S:S + 4 * R]
        zt_ps = y_ps[:, :].bitcast(bf16)

        x_in = [sem(f"x_in{r}") for r in range(RING)]
        c_in = [sem(f"c_in{r}") for r in range(RING)]
        stored = sem("stored")
        consts_in, rows_in, ffn_in = sem("consts_in"), sem("rows_in"), sem("ffn_in")
        pool_set, gate_w_turned, dve_set = sem("pool_set"), sem("gate_w_turned"), sem("dve_set")
        v_norm = Stage(sem("v_norm"), "bn0 bn1 mv0 mv1 rq nb")
        a_norm = Stage(sem("a_norm"), "log r q0 q1")
        t_turn = Stage(sem("t_turn"), "r0 r1 r2 r3 gates")
        a_turn = Stage(sem("a_turn"), "r0 r1 r2 r3 gates")
        t_scan = Stage(sem("t_scan"), "rows turned", GROUP)
        v_scan = Stage(sem("v_scan"), "z neg abs ncs a m ex0 ex1 ex2 negm p1 rest p2 p2b p3", GROUP)
        a_scan = Stage(sem("a_scan"), "exp log ex facs", GROUP)
        v_val = Stage(sem("v_val"), "sum mean")
        p_val = Stage(sem("p_val"), "val0 val1")
        t_attn = Stage(sem("t_attn"), "arg0 qk0 arg1 st0 st1 qk1 pv0 arg2 pv1 qk2 in0 in1 arg3 pv2 qk3 pv3")
        a_attn = Stage(sem("a_attn"), "exp0 exp1 st0 st1 g0 exp2 g1 exp3")
        p_attn = Stage(sem("p_attn"), "kw0 mask0 kw1 mask1 mask2 mask3")
        v_attn = Stage(sem("v_attn"), "c0 c1 c2 in0 in1 c3 g2 g3")
        a_mix = Stage(sem("a_mix"), "sq hlog hr log r z0 z1")
        v_mix = Stage(sem("v_mix"), "ss n0 n n1 n2 v vc hn x1 bn0 bn1 mv0 mv1 nb")
        p_mix = Stage(sem("p_mix"), "hw")
        t_ffn = Stage(sem("t_ffn"), "zt y0 y1")
        a_ffn = Stage(sem("a_ffn"), "zq y0 y1")
        v_ffn = Stage(sem("v_ffn"), "yb")
        p_ffn = Stage(sem("p_ffn"), "out")

        block = es.enter_context(nc.Block())

        def slots(eng, slot):
            for k in range(-5, RING):
                slot(Batch(0, k))
            with eng.Fori(1, B // RING - 1) as it:
                for k in range(RING):
                    slot(Batch(it, k))
            for k in range(RING + 2):
                slot(Batch(B // RING - 1, k))

        def scans(m):
            return (m + 1).k % GROUP == 0 and (m + 1).exists(B)

        def heads(ap):
            return ap.rearrange("p (h d) -> p h d", d=DH)

        N_CONSTS = 16 * (3 + 2 * GROUP + 2)
        N_POOL_SET, N_DVE_SET = 4, 8 + 9 * C

        @block.sync
        def _(sp):
            def rows_of(t, b):
                return t[bass.ds(b.index, 1), :, :].rearrange("o (t p) e -> p (o t) e", p=P)

            def load(b):
                r = b.k % RING
                if b.follows(RING):
                    sp.wait_ge(v_mix.sem, v_mix.at(b - RING, "x1"))
                sp.dma_start(x_sb[:, r, :, :], rows_of(x, b)).then_inc(x_in[r], 16)
                if b.follows(RING):
                    sp.wait_ge(p_attn.sem, p_attn.at(b - RING, "kw1"))
                sp.dma_start(c_sb[:, r, :, :], rows_of(ctx, b)).then_inc(c_in[r], 16)

            sp.dma_start(ident[:, :], c_ident).then_inc(consts_in, 16)
            sp.dma_start(w_rows[0:NH, :], igate_w).then_inc(rows_in, 16)
            sp.dma_start(w_rows[NH:2 * NH, :], fgate_w).then_inc(rows_in, 16)
            sp.dma_start(w_ffn[:, :, :], ffn_w.rearrange("(c p) f -> p c f", p=P)).then_inc(ffn_in, 16)
            for col, s in ((0, s_in), (1, s_k)):
                sp.dma_start(sc[:, col:col + 1], s.partition_broadcast(P)).then_inc(ffn_in, 16)
            load(Batch(0, 0))
            load(Batch(0, 1))
            sp.dma_start(gsel[:, :, :], c_gsel).then_inc(consts_in, 16)
            sp.dma_start(hsel_f[:, :], c_hsel).then_inc(consts_in, 16)
            for j in range(GROUP):
                for dst, src in ((b_i, igate_b), (b_f, fgate_b)):
                    sp.dma_start(dst[j * NH:(j + 1) * NH, :],
                                 src.rearrange("(h o) -> h o", o=1)).then_inc(consts_in, 16)
            sp.dma_start(w_out[:, :], out_w.partition_broadcast(P)).then_inc(consts_in, 16)
            sp.dma_start(b_ffn[:, :], bias.partition_broadcast(P)).then_inc(consts_in, 16)

            def slot(m):
                if (m + 7).exists(B):
                    load(m + 7)
                if (m - 2).exists(B):
                    sp.wait_ge(p_ffn.sem, p_ffn.at(m - 2, "out"))
                    sp.dma_start(rows_of(out, m - 2), o_sb[:, :, :]).then_inc(stored, 16)

            slots(sp, slot)
            sp.wait_ge(stored, 16 * B)

        @block.tensor
        def _(pe):
            mm, turn = nc.tensor.matmul, nc.tensor.transpose

            pe.wait_ge(consts_in, N_CONSTS)
            pe.wait_ge(rows_in, 32)
            for i in range(3 * C):
                last = turn(gate_ps[:, i * 2 * NH:(i + 1) * 2 * NH], w_rows[:, i * P:(i + 1) * P],
                            ident[0:2 * NH, 0:2 * NH])
            last.then_inc(gate_w_turned, 1)
            pe.wait_ge(dve_set, N_DVE_SET)
            pe.wait_ge(pool_set, N_POOL_SET)

            def turn_round(b, i):
                if i == 0:
                    pe.wait_ge(a_norm.sem, a_norm.at(b, "q1"))
                if i == 2:
                    pe.wait_ge(c_in[b.k % RING], b.count(16, 16, RING))
                if i >= 2:
                    pe.wait_ge(a_turn.sem, a_turn.at(b, f"r{i - 2}"))
                elif b.follows(1):
                    pe.wait_ge(a_turn.sem, a_turn.at(b - 1, f"r{i + 2}"))
                for c in range(2):
                    for t in range(T):
                        chunk = slice((2 * (i % 2) + c) * P, (2 * (i % 2) + c + 1) * P)
                        src = q_nat[:, t, chunk] if i < 2 else c_sb[:, b.k % RING, t, chunk]
                        last = turn(turn_ps[i % 2][:, (T * c + t) * P:(T * c + t + 1) * P], src, ident[:, :])
                last.then_inc(t_turn.sem, 1)

            def gates(b):
                r = b.k % RING
                pe.wait_ge(a_turn.sem, a_turn.at(b, "r3"))
                if b.follows(1):
                    pe.wait_ge(a_turn.sem, a_turn.at(b - 1, "gates"))
                for w, src, first in ((w_x, qT, True), (w_c, kT, False)):
                    for c in range(C):
                        last = mm(part_ps[32 * c:32 * c + 32, :], w[:, c, :], src[:, r, c, :],
                                  start=first, stop=not first)
                last.then_inc(t_turn.sem, 1)

            def scan_rows(b):
                pe.wait_ge(a_turn.sem, a_turn.at(b + (GROUP - 1), "gates"))
                if b.follows(GROUP):
                    pe.wait_ge(a_scan.sem, a_scan.at(b - GROUP, "facs"))
                for j in range(GROUP):
                    last = mm(rows_ps, gsel[:, j, :], g_part[:, j, :], start=j == 0, stop=j == GROUP - 1)
                last.then_inc(t_scan.sem, 1)

            def scan_turned(b):
                for i in range(4):
                    last = turn(facs_ps[:, i * R:(i + 1) * R], ex[:, i * P:(i + 1) * P], ident[0:R, 0:R])
                last.then_inc(t_scan.sem, 1)

            def arg(b, q):
                t, u, j, g = q // U, q % U, b.k % GROUP, b.k // GROUP % 2
                row = j * NH + u
                if q == 0:
                    pe.wait_ge(v_scan.sem, v_scan.at(b, "p3"))
                if q:
                    pe.wait_ge(a_attn.sem, a_attn.at(b, f"exp{q - 1}"))
                elif b.follows(1):
                    pe.wait_ge(a_attn.sem, a_attn.at(b - 1, "exp3"))
                mm(arg_ps[:, :], split[:, g, t * P:(t + 1) * P], hsel[:, row:row + NH - 1:2].unsqueeze(2).broadcast_to([3 * R, 4, P]),
                   start=True, stop=False)
                for h in range(4):
                    last = mm(arg_ps[:, h * P:(h + 1) * P], hsel[:, row + 2 * h:row + 2 * h + 1].broadcast_to([3 * R, P]),
                              split[:, g, S + t * P:S + (t + 1) * P], start=False, stop=h == 3)
                last.then_inc(t_attn.sem, 1)

            def scores(b, q):
                t, u, r = q // U, q % U, b.k % RING
                if q:
                    pe.wait_ge(v_attn.sem, v_attn.at(b, f"c{q - 1}"))
                elif b.follows(1):
                    pe.wait_ge(v_attn.sem, v_attn.at(b - 1, "c3"))
                half = slice(DH * u, DH * u + DH)
                for c in range(C):
                    last = mm(qk_ps[:, c * P:(c + 1) * P], kT[half, r, c, t * P:(t + 1) * P],
                              qT[half, r, c, t * P:(t + 1) * P], start=True, stop=True)
                last.then_inc(t_attn.sem, 1)

            def states(b, u):
                if u == 0:
                    pe.wait_ge(p_attn.sem, p_attn.at(b, "kw1"))
                    pe.wait_ge(p_val.sem, p_val.at(b, "val1"))
                if b.follows(1):
                    pe.wait_ge(v_attn.sem, v_attn.at(b - 1, f"g{2 + u}"))
                for i in range(2):
                    pair = 2 * u + i
                    last = mm(work_ps[u][:, i * 2 * W:(i + 1) * 2 * W], k_w[:, pair * P:(pair + 1) * P],
                              val[:, b.k % 2, 2 * pair:2 * pair + 2, :], start=True, stop=True)
                last.then_inc(t_attn.sem, 1)

            def within(b, q):
                t, u = q // U, q % U
                pe.wait_ge(v_attn.sem, v_attn.at(b, ("c0", "c1", "in0", "c3")[q]))
                if t == 0:
                    pe.wait_ge(a_attn.sem, a_attn.at(b, f"st{u}"))
                for h in range(4):
                    last = mm(work_ps[u][:, h * W:(h + 1) * W], dec[:, q, h * P:(h + 1) * P],
                              val[:, b.k % 2, t * NH + 2 * h + u, :], start=True, stop=True)
                last.then_inc(t_attn.sem, 1)

            def across(b, u):
                pe.wait_ge(a_attn.sem, a_attn.at(b, f"g{u}"))
                for i in range(2):
                    last = mm(work_ps[u][:, i * 2 * W:(i + 1) * 2 * W], qT[:, b.k % RING, 2 * u + i, P:2 * P],
                              state[:, u, i, :], start=True, stop=True)
                last.then_inc(t_attn.sem, 1)

            def ffn_turn(b):
                pe.wait_ge(a_mix.sem, a_mix.at(b, "z1"))
                if b.follows(1):
                    pe.wait_ge(a_ffn.sem, a_ffn.at(b - 1, "y1"))
                for c in range(C):
                    for t in range(T):
                        last = turn(zt_ps[:, c * S + t * P:c * S + (t + 1) * P],
                                    z_bf[:, t, c * P:(c + 1) * P], ident_bf[:, :])
                last.then_inc(t_ffn.sem, 1)

            def ffn(b, t):
                for c in range(C):
                    last = mm(y_ps[:, :], zq[:, c, t * P:(t + 1) * P], w_ffn[:, c, :],
                              start=c == 0, stop=c == C - 1)
                last.then_inc(t_ffn.sem, 1)

            def slot(m):
                turning, attending, feeding = ((m + d).exists(B) for d in (4, 0, -2))
                if turning:
                    turn_round(m + 4, 0)
                    turn_round(m + 4, 1)
                if attending:
                    arg(m, 0)
                    scores(m, 0)
                if turning:
                    turn_round(m + 4, 2)
                    turn_round(m + 4, 3)
                if attending:
                    arg(m, 1)
                    states(m, 0)
                    states(m, 1)
                    scores(m, 1)
                if turning:
                    gates(m + 4)
                if attending:
                    within(m, 0)
                if scans(m):
                    scan_rows(m + 1)
                if attending:
                    arg(m, 2)
                if feeding:
                    ffn_turn(m - 2)
                if attending:
                    within(m, 1)
                    scores(m, 2)
                    across(m, 0)
                if feeding:
                    pe.wait_ge(a_ffn.sem, a_ffn.at(m - 2, "zq"))
                if attending:
                    across(m, 1)
                if feeding:
                    ffn(m - 2, 0)
                if attending:
                    arg(m, 3)
                    within(m, 2)
                    scores(m, 3)
                if scans(m):
                    pe.wait_ge(a_scan.sem, a_scan.at(m + 1, "ex"))
                if feeding:
                    pe.wait_ge(a_ffn.sem, a_ffn.at(m - 2, "y0"))
                if attending:
                    within(m, 3)
                if scans(m):
                    scan_turned(m + 1)
                if feeding:
                    ffn(m - 2, 1)

            slots(pe, slot)

        @block.scalar
        def _(act):
            af = nc.scalar.activation
            nc.scalar.preload_act_table_set("natural_log_exp_and_others")
            act.wait_ge(dve_set, N_DVE_SET)
            act.wait_ge(pool_set, N_POOL_SET)

            def turned(b, i):
                act.wait_ge(t_turn.sem, t_turn.at(b, f"r{i}"))
                dst = (qT if i < 2 else kT)[:, b.k % RING, 2 * (i % 2):2 * (i % 2) + 2, :]
                af(dst.rearrange("p c s -> p (c s)"), turn_ps[i % 2][:, :], ACT.Copy).then_inc(a_turn.sem, 1)

            def gates(b):
                act.wait_ge(t_turn.sem, t_turn.at(b, "gates"))
                af(g_part[:, b.k % GROUP, :], part_ps, ACT.Copy).then_inc(a_turn.sem, 1)

            def decay(b, q):
                act.wait_ge(t_attn.sem, t_attn.at(b, f"arg{q}"))
                af(dec[:, q, :], arg_ps[:, :], ACT.Exp).then_inc(a_attn.sem, 1)

            def keep_states(b):
                for u in range(U):
                    act.wait_ge(t_attn.sem, t_attn.at(b, f"st{u}"))
                    src = work_ps[u][:, 0:4 * W].rearrange("p (i w) -> p i w", i=2)
                    af(state[0:DH, u, :, 0:W], src[0:DH, :, 0:W], ACT.Copy)
                    af(state[DH:P, u, :, W:2 * W], src[DH:P, :, W:2 * W], ACT.Copy).then_inc(a_attn.sem, 1)

            def keep_tile0(b, u):
                act.wait_ge(t_attn.sem, t_attn.at(b, f"pv{u}"))
                if b.follows(2):
                    act.wait_ge(v_mix.sem, v_mix.at(b - 2, "hn"))
                af(g_sb[:, b.k % 2, u:NH:2, :], work_ps[u][:, 0:4 * W].rearrange("p (h w) -> p h w", w=W),
                   ACT.Copy).then_inc(a_attn.sem, 1)

            def norm_rstd(b):
                act.wait_ge(v_norm.sem, v_norm.at(b, "mv1"))
                af(log1[:, :], mv1[:, :, 1], ACT.Ln, bias=ln_eps[:, :]).then_inc(a_norm.sem, 1)
                act.wait_ge(a_norm.sem, a_norm.at(b, "log"))
                af(r1[:, :], log1[:, :], ACT.Exp, scale=-0.5).then_inc(a_norm.sem, 1)

            def norm_apply(b):
                act.wait_ge(v_norm.sem, v_norm.at(b, "nb"))
                if b.follows(1):
                    act.wait_ge(t_turn.sem, t_turn.at(b - 1, "r1"))
                for t in range(T):
                    af(q_nat[:, t, :], x_sb[:, b.k % RING, t, :], ACT.Identity, bias=nb1[:, t:t + 1],
                       scale=r1q[:, t:t + 1]).then_inc(a_norm.sem, 1)

            def scan_softplus(b):
                act.wait_ge(v_scan.sem, v_scan.at(b, "abs"))
                af(z_abs[:, :], z_abs[:, :], ACT.Exp, scale=-1.0).then_inc(a_scan.sem, 1)
                act.wait_ge(a_scan.sem, a_scan.at(b, "exp"))
                af(z_abs[:, :], z_abs[:, :], ACT.Ln, bias=1.0).then_inc(a_scan.sem, 1)

            def scan_exps(b):
                act.wait_ge(v_scan.sem, v_scan.at(b, "ex2"))
                af(ex[:, :], ex[:, :], ACT.Exp).then_inc(a_scan.sem, 1)

            def scan_facs(b):
                act.wait_ge(t_scan.sem, t_scan.at(b, "turned"))
                af(facs[:, b.k // GROUP % 2, :, :].rearrange("p k r -> p (k r)"), facs_ps,
                   ACT.Copy).then_inc(a_scan.sem, 1)

            def squares(b):
                act.wait_ge(v_attn.sem, v_attn.at(b, "g3"))
                act.wait_ge(a_attn.sem, a_attn.at(b, "g1"))
                if b.follows(2):
                    act.wait_ge(p_ffn.sem, p_ffn.at(b - 2, "out"))
                af(x1[:, b.k % 2, :, :].rearrange("p t (h d) -> p (t h) d", d=DH),
                   g_sb[:, b.k % 2, :, 0:DH], ACT.Square).then_inc(a_mix.sem, 1)

            def head_rstd(b):
                act.wait_ge(v_mix.sem, v_mix.at(b, "vc"))
                af(h_log[:, :], h_vc[:, :], ACT.Ln).then_inc(a_mix.sem, 1)
                act.wait_ge(a_mix.sem, a_mix.at(b, "hlog"))
                af(h_r[:, :], h_log[:, :], ACT.Exp, scale=-0.5).then_inc(a_mix.sem, 1)

            def mix_rstd(b):
                act.wait_ge(v_mix.sem, v_mix.at(b, "mv1"))
                af(log2[:, :], mv2[:, :, 1], ACT.Ln, bias=ln_eps[:, :]).then_inc(a_mix.sem, 1)
                act.wait_ge(a_mix.sem, a_mix.at(b, "log"))
                af(r2[:, :], log2[:, :], ACT.Exp, scale=-0.5).then_inc(a_mix.sem, 1)

            def mix_apply(b):
                act.wait_ge(v_mix.sem, v_mix.at(b, "nb"))
                if b.follows(1):
                    act.wait_ge(t_ffn.sem, t_ffn.at(b - 1, "zt"))
                for t in range(T):
                    af(z_bf[:, t, :], x1[:, b.k % 2, t, :], ACT.Identity, bias=nb2[:, t:t + 1],
                       scale=r2[:, t:t + 1]).then_inc(a_mix.sem, 1)

            def quantise(b):
                af(zq[:, :, :].rearrange("p c s -> p (c s)"), zt_ps, ACT.Copy, scale=s_inv[:, 0:1],
                   saturate=False).then_inc(a_ffn.sem, 1)

            def dequantise(b, t):
                act.wait_ge(t_ffn.sem, t_ffn.at(b, f"y{t}"))
                if t == 0:
                    if b.follows(1):
                        act.wait_ge(p_ffn.sem, p_ffn.at(b - 1, "out"))
                af(y_bf[:, t, :], y_ps[:, :], ACT.Copy, scale=s_out[:, :]).then_inc(a_ffn.sem, 1)

            def slot(m):
                norming, turning, attending, mixing, feeding = ((m + d).exists(B) for d in (5, 4, 0, -1, -2))
                if turning:
                    turned(m + 4, 0)
                    turned(m + 4, 1)
                if attending:
                    decay(m, 0)
                if mixing:
                    squares(m - 1)
                if turning:
                    turned(m + 4, 2)
                    turned(m + 4, 3)
                if attending:
                    decay(m, 1)
                    keep_states(m)
                if norming:
                    norm_rstd(m + 5)
                if mixing:
                    head_rstd(m - 1)
                if turning:
                    gates(m + 4)
                if attending:
                    keep_tile0(m, 0)
                if feeding:
                    act.wait_ge(t_ffn.sem, t_ffn.at(m - 2, "zt"))
                if attending:
                    decay(m, 2)
                if feeding:
                    quantise(m - 2)
                if scans(m):
                    scan_softplus(m + 1)
                if attending:
                    keep_tile0(m, 1)
                if norming:
                    norm_apply(m + 5)
                if feeding:
                    dequantise(m - 2, 0)
                if attending:
                    decay(m, 3)
                if scans(m):
                    scan_exps(m + 1)
                if mixing:
                    mix_rstd(m - 1)
                if feeding:
                    dequantise(m - 2, 1)
                if mixing:
                    mix_apply(m - 1)
                if scans(m):
                    scan_facs(m + 1)

            slots(act, slot)

        @block.vector
        def _(dve):
            ve = nc.vector
            tt, ts, stt = ve.tensor_tensor, ve.tensor_scalar, ve.scalar_tensor_tensor
            done = [0]

            def setup(ins):
                done[0] += 1
                ins.then_inc(dve_set, 1)
                dve.wait_ge(dve_set, done[0])

            dve.wait_ge(pool_set, N_POOL_SET)
            setup(ve.memset(ln_eps[:, :], LN_EPS))
            dve.wait_ge(consts_in, N_CONSTS)
            setup(ve.tensor_copy(ident_bf[:, :], ident[:, :]))
            setup(ve.tensor_copy(hsel[:, :], hsel_f[:, :]))
            dve.wait_ge(gate_w_turned, 1)
            turned = gate_ps[:, 0:3 * C * 2 * NH].rearrange("p (k c g) -> p k c g", k=3, c=C)
            setup(ts(w_x[:, :, 0:2 * NH], turned[:, 0, :, :], 1.0 / Q_SCALE, None, ALU.mult))
            setup(ve.tensor_copy(w_c[:, :, 0:2 * NH], turned[:, 1, :, :]))
            setup(tt(w_c[:, :, 0:2 * NH], turned[:, 2, :, :], w_c[:, :, 0:2 * NH], ALU.add))
            dve.wait_ge(ffn_in, 48)
            setup(ve.reciprocal(s_inv[:, :], sc[:, :]))
            setup(tt(s_out[:, :], sc[:, 0:1], sc[:, 1:2], ALU.mult))
            for c in range(C):
                setup(ts(f_val, w_ffn[:, c, :], s_inv[:, 1:2], None, ALU.mult))
                setup(ts(f_mag.bitcast(i32), f_val.bitcast(i32), 0x7F800000, None, ALU.bitwise_and))
                setup(ts(f_mag, f_mag, 2.0 ** -6, 1.5 * 2.0 ** 20, ALU.max, ALU.mult))
                setup(tt(f_tmp, f_val, f_mag, ALU.add))
                setup(tt(f_val, f_tmp, f_mag, ALU.subtract))
                setup(stt(f_tmp, f_val, -1.0, f_val, ALU.mult, ALU.max))
                setup(ts(f_tmp, f_tmp, 448.0, 3e38, ALU.is_gt, ALU.mult))
                setup(ts(f_mag, f_tmp, 3e38, None, ALU.mult))
                setup(stt(w_ffn[:, c, :], f_mag, 0.0, f_val, ALU.mult, ALU.add))
            assert done[0] == N_DVE_SET

            def norm_stats(b):
                r = b.k % RING
                dve.wait_ge(x_in[r], b.count(16, 16, RING))
                for t in range(T):
                    ve.bn_stats(bn1[:, t, :], x_sb[:, r, t, :]).then_inc(v_norm.sem, 1)

            def norm_moments(b):
                for t in range(T):
                    ve.bn_aggr(mv1[:, t, :], bn1[:, t, :]).then_inc(v_norm.sem, 1)

            def norm_scale(b):
                dve.wait_ge(a_norm.sem, a_norm.at(b, "r"))
                ts(r1q[:, :], r1[:, :], Q_SCALE, None, ALU.mult).then_inc(v_norm.sem, 1)
                dve.wait_ge(v_norm.sem, v_norm.at(b, "rq"))
                stt(nb1[:, :], mv1[:, :, 0], -1.0, r1q[:, :], ALU.mult, ALU.mult).then_inc(v_norm.sem, 1)

            def value_means(b):
                r = b.k % RING
                dve.wait_ge(c_in[r], b.count(16, 16, RING))
                ve.tensor_reduce(v_sum[:, :], c_sb[:, r, :, :].rearrange("p t (h d) -> p (t h) d", d=DH),
                                 AX.X, ALU.add).then_inc(v_val.sem, 1)
                dve.wait_ge(v_val.sem, v_val.at(b, "sum"))
                if b.follows(1):
                    dve.wait_ge(p_val.sem, p_val.at(b - 1, "val1"))
                ts(v_mean[:, :], v_sum[:, :], 1.0 / DH, None, ALU.mult).then_inc(v_val.sem, 1)

            def matrix(b, q):
                dve.wait_ge(t_attn.sem, t_attn.at(b, f"qk{q}"))
                dve.wait_ge(p_attn.sem, p_attn.at(b, f"mask{q}"))
                tt(dec[:, q, :], qk_ps[:, :], dec[:, q, :], ALU.mult).then_inc(v_attn.sem, 1)

            def carried(b, u):
                row, g = b.k % GROUP * NH + 4 * u, b.k // GROUP % 2
                dve.wait_ge(t_attn.sem, t_attn.at(b, f"in{u}"))
                tt(carry[:, 4 * u:4 * u + 4, :], work_ps[u][:, 0:4 * W].rearrange("p (h w) -> p h w", w=W),
                   facs[:, g, 2, row:row + 4].unsqueeze(2).broadcast_to([P, 4, W]),
                   ALU.mult).then_inc(v_attn.sem, 1)

            def keep_tile1(b, u):
                dve.wait_ge(t_attn.sem, t_attn.at(b, f"pv{2 + u}"))
                dve.wait_ge(v_attn.sem, v_attn.at(b, "in1"))
                tt(g_sb[:, b.k % 2, NH + u:2 * NH:2, :], work_ps[u][:, 0:4 * W].rearrange("p (h w) -> p h w", w=W),
                   carry[:, u:NH:2, :], ALU.add).then_inc(v_attn.sem, 1)

            def head_var(b):
                dve.wait_ge(a_mix.sem, a_mix.at(b, "sq"))
                ve.tensor_reduce(g_ss[:, :], x1[:, b.k % 2, :, :].rearrange("p t (h d) -> p (t h) d", d=DH),
                                 AX.X, ALU.add).then_inc(v_mix.sem, 1)
                dve.wait_ge(v_attn.sem, v_attn.at(b, "g3"))
                row, g = b.k % GROUP * NH, b.k // GROUP % 2
                sums = g_sb[:, b.k % 2, :, DH].rearrange("p (t h) -> p t h", t=T)
                stt(h_n0[:, :, :], sums, -1.0, facs[:, g, 0:T, row:row + NH], ALU.mult,
                    ALU.max).then_inc(v_mix.sem, 1)
                dve.wait_ge(v_mix.sem, v_mix.at(b, "n0"))
                tt(h_n[:, :, :], h_n0[:, :, :], sums, ALU.max).then_inc(v_mix.sem, 1)
                dve.wait_ge(v_mix.sem, v_mix.at(b, "n"))
                ts(h_n1[:, :], h_n[:, :, :].rearrange("p t h -> p (t h)"), EPS, None, ALU.add).then_inc(v_mix.sem, 1)
                dve.wait_ge(v_mix.sem, v_mix.at(b, "n1"))
                stt(h_n2[:, :], h_n1[:, :], LN_EPS, h_n1[:, :], ALU.mult, ALU.mult).then_inc(v_mix.sem, 1)
                dve.wait_ge(v_mix.sem, v_mix.at(b, "n2"))
                stt(h_v[:, :], g_ss[:, :], 1.0 / DH, h_n2[:, :], ALU.mult, ALU.add).then_inc(v_mix.sem, 1)
                dve.wait_ge(v_mix.sem, v_mix.at(b, "v"))
                ts(h_vc[:, :], h_v[:, :], TOP, None, ALU.min).then_inc(v_mix.sem, 1)

            def head_norm(b):
                dve.wait_ge(a_mix.sem, a_mix.at(b, "hr"))
                tt(x1[:, b.k % 2, :, :].rearrange("p t (h d) -> p (t h) d", d=DH), g_sb[:, b.k % 2, :, 0:DH],
                   h_r[:, :].unsqueeze(2).broadcast_to([P, T * NH, DH]), ALU.mult).then_inc(v_mix.sem, 1)

            def residual(b):
                dve.wait_ge(p_mix.sem, p_mix.at(b, "hw"))
                tt(x1[:, b.k % 2, :, :], x1[:, b.k % 2, :, :], x_sb[:, b.k % RING, :, :],
                   ALU.add).then_inc(v_mix.sem, 1)

            def mix_stats(b):
                dve.wait_ge(v_mix.sem, v_mix.at(b, "x1"))
                for t in range(T):
                    ve.bn_stats(bn2[:, t, :], x1[:, b.k % 2, t, :]).then_inc(v_mix.sem, 1)

            def mix_moments(b):
                for t in range(T):
                    ve.bn_aggr(mv2[:, t, :], bn2[:, t, :]).then_inc(v_mix.sem, 1)

            def mix_scale(b):
                dve.wait_ge(a_mix.sem, a_mix.at(b, "r"))
                stt(nb2[:, :], mv2[:, :, 0], -1.0, r2[:, :], ALU.mult, ALU.mult).then_inc(v_mix.sem, 1)

            def add_bias(b):
                dve.wait_ge(a_ffn.sem, a_ffn.at(b, "y1"))
                tt(y_bf[:, :, :], y_bf[:, :, :], b_ffn[:, :].unsqueeze(1).broadcast_to([P, T, F]),
                   ALU.add).then_inc(v_ffn.sem, 1)

            def scan_gate(b):
                dve.wait_ge(t_scan.sem, t_scan.at(b, "rows"))
                ts(z_f, rows_ps[R:2 * R, :], b_f[:, :], None, ALU.add).then_inc(v_scan.sem, 1)
                dve.wait_ge(v_scan.sem, v_scan.at(b, "z"))
                ts(z_neg, z_f, -1.0, 0.0, ALU.mult, ALU.max).then_inc(v_scan.sem, 1)
                stt(z_abs[:, :], z_f, -1.0, z_f, ALU.mult, ALU.max).then_inc(v_scan.sem, 1)

            def scan_sums(b):
                dve.wait_ge(a_scan.sem, a_scan.at(b, "log"))
                ve.tensor_tensor_scan(ncs[:, :], z_abs[:, :], z_neg, 0.0, ALU.add,
                                      ALU.add).then_inc(v_scan.sem, 1)
                dve.wait_ge(v_scan.sem, v_scan.at(b, "ncs"))
                stt(am[:, 0:S], rows_ps[0:R, :], b_i[:, :], ncs[:, :], ALU.add, ALU.add).then_inc(v_scan.sem, 1)
                dve.wait_ge(v_scan.sem, v_scan.at(b, "a"))
                ve.tensor_tensor_scan(mx[:, :], am[:, 0:S], am[:, 0:S], -3.0e38, ALU.max,
                                      ALU.max).then_inc(v_scan.sem, 1)
                dve.wait_ge(v_scan.sem, v_scan.at(b, "m"))
                tt(ex[:, 0:S], ncs[:, :], mx[:, :], ALU.subtract).then_inc(v_scan.sem, 1)
                ts(ex[:, S:S + P], mx[:, P:S], -1.0, mx[:, P - 1:P], ALU.mult, ALU.add).then_inc(v_scan.sem, 1)
                ts(ex[:, S + P:2 * S], am[:, 0:P], mx[:, P - 1:P], None, ALU.subtract).then_inc(v_scan.sem, 1)

            def scan_split(b):
                g = b.k // GROUP % 2
                ts(am[:, S:2 * S], mx[:, :], -1.0, None, ALU.mult).then_inc(v_scan.sem, 1)
                dve.wait_ge(v_scan.sem, v_scan.at(b, "negm"))
                ve.tensor_copy(split[0:R, g, :], am[:, :]).then_inc(v_scan.sem, 1)
                dve.wait_ge(v_scan.sem, v_scan.at(b, "p1"))
                tt(rest[:, :], am[:, :], split[0:R, g, :], ALU.subtract).then_inc(v_scan.sem, 1)
                dve.wait_ge(v_scan.sem, v_scan.at(b, "rest"))
                ve.tensor_copy(part2[:, :], rest[:, :]).then_inc(v_scan.sem, 1)
                dve.wait_ge(v_scan.sem, v_scan.at(b, "p2"))
                ve.tensor_copy(split[R:2 * R, g, :], part2[:, :]).then_inc(v_scan.sem, 1)
                tt(split[2 * R:3 * R, g, :], rest[:, :], part2[:, :], ALU.subtract).then_inc(v_scan.sem, 1)

            def slot(m):
                norming, valuing, attending, mixing, feeding = ((m + d).exists(B) for d in (5, 1, 0, -1, -2))
                if norming:
                    norm_stats(m + 5)
                    dve.wait_ge(v_norm.sem, v_norm.at(m + 5, "bn1"))
                if attending:
                    matrix(m, 0)
                if norming:
                    norm_moments(m + 5)
                if mixing:
                    head_var(m - 1)
                if attending:
                    matrix(m, 1)
                if norming:
                    norm_scale(m + 5)
                if mixing:
                    head_norm(m - 1)
                if valuing:
                    value_means(m + 1)
                if scans(m):
                    scan_gate(m + 1)
                if attending:
                    matrix(m, 2)
                if scans(m):
                    scan_sums(m + 1)
                if attending:
                    carried(m, 0)
                    carried(m, 1)
                if mixing:
                    residual(m - 1)
                    mix_stats(m - 1)
                    dve.wait_ge(v_mix.sem, v_mix.at(m - 1, "bn1"))
                if attending:
                    matrix(m, 3)
                if mixing:
                    mix_moments(m - 1)
                if feeding:
                    add_bias(m - 2)
                if attending:
                    keep_tile1(m, 0)
                if scans(m):
                    scan_split(m + 1)
                if mixing:
                    mix_scale(m - 1)
                if attending:
                    keep_tile1(m, 1)

            slots(dve, slot)

        @block.gpsimd
        def _(pool):
            pl = nc.gpsimd
            pl.memset(val[:, :, :, DH:W], 1.0).then_inc(pool_set, 1)
            pl.memset(state[:, :, :, :], 0.0).then_inc(pool_set, 1)
            pl.memset(w_x[:, :, :], 0.0).then_inc(pool_set, 1)
            pl.memset(w_c[:, :, :], 0.0).then_inc(pool_set, 1)
            pool.wait_ge(consts_in, N_CONSTS)

            def weigh_keys(b, u):
                row, g, some = b.k % GROUP * NH + 4 * u, b.k // GROUP % 2, slice(4 * u, 4 * u + 4)
                if u == 0:
                    pool.wait_ge(a_scan.sem, a_scan.at(b, "facs"))
                    pool.wait_ge(c_in[b.k % RING], b.count(16, 16, RING))
                    if b.follows(1):
                        pool.wait_ge(t_attn.sem, t_attn.at(b - 1, "st1"))
                pool.wait_ge(a_attn.sem, a_attn.at(b, f"exp{u}"))
                pl.tensor_tensor(heads(k_w[:, :])[:, some, :], heads(c_sb[:, b.k % RING, 0, :])[:, some, :],
                                 facs[:, g, 3, row:row + 4].unsqueeze(2).broadcast_to([P, 4, DH]),
                                 ALU.mult).then_inc(p_attn.sem, 1)

            def mask(b, q):
                pl.affine_select(out=dec[:, q, :], in_=dec[:, q, :], compare_op=ALU.is_ge, fill=0.0, base=0,
                                 pattern=[[0, 4], [1, P]], channel_multiplier=-1).then_inc(p_attn.sem, 1)

            def scale_heads(b):
                pool.wait_ge(v_mix.sem, v_mix.at(b, "hn"))
                h = x1[:, b.k % 2, :, :]
                pl.tensor_tensor(h, h, w_out[:, :].unsqueeze(1).broadcast_to([P, T, E]),
                                 ALU.mult).then_inc(p_mix.sem, 1)

            def centre_values(b, t):
                if t == 0:
                    pool.wait_ge(v_val.sem, v_val.at(b, "mean"))
                    if b.follows(2):
                        pool.wait_ge(t_attn.sem, t_attn.at(b - 2, "pv3"))
                pl.tensor_tensor(val[:, b.k % 2, t * NH:(t + 1) * NH, 0:DH], heads(c_sb[:, b.k % RING, t, :]),
                                 v_mean[:, t * NH:(t + 1) * NH].unsqueeze(2).broadcast_to([P, NH, DH]),
                                 ALU.subtract).then_inc(p_val.sem, 1)

            def output(b):
                pool.wait_ge(v_ffn.sem, v_ffn.at(b, "yb"))
                if b.follows(1):
                    pool.wait_ge(stored, b.count(16, 0))
                pl.tensor_tensor(o_sb[:, :, :], x1[:, b.k % 2, :, :], y_bf[:, :, :],
                                 ALU.add).then_inc(p_ffn.sem, 1)

            def slot(m):
                valuing, attending, mixing, feeding = ((m + d).exists(B) for d in (1, 0, -1, -2))
                if attending:
                    weigh_keys(m, 0)
                    mask(m, 0)
                    weigh_keys(m, 1)
                    mask(m, 1)
                    pool.wait_ge(a_attn.sem, a_attn.at(m, "exp2"))
                if mixing:
                    scale_heads(m - 1)
                if attending:
                    mask(m, 2)
                if valuing:
                    centre_values(m + 1, 0)
                if attending:
                    pool.wait_ge(a_attn.sem, a_attn.at(m, "exp3"))
                if valuing:
                    centre_values(m + 1, 1)
                if attending:
                    mask(m, 3)
                if feeding:
                    output(m - 2)

            slots(pool, slot)


def shape_constants(n_heads):
    import numpy as np
    rows = GROUP * n_heads
    ident = np.eye(P, dtype=np.float32)
    gsel = np.zeros((P, GROUP, 2 * rows), np.float32)
    for chunk in range(P // 32):
        for j in range(GROUP):
            for h in range(n_heads):
                gsel[32 * chunk + h, j, j * n_heads + h] = 1
                gsel[32 * chunk + n_heads + h, j, rows + j * n_heads + h] = 1
    hsel = np.zeros((3 * rows, rows), np.float32)
    for part in range(3):
        for row in range(rows):
            hsel[part * rows + row, row] = 1
    return {"c_ident": ident, "c_gsel": gsel, "c_hsel": hsel}


INPUTS = ["x", "ctx_1024", "L0_xattn_igate_w", "L0_xattn_igate_b", "L0_xattn_fgate_w", "L0_xattn_fgate_b",
          "L0_xattn_out_w", "L0_ffn_kernel", "L0_ffn_input_scale", "L0_ffn_kernel_scale", "L0_ffn_bias"]


def kernel(**inputs):
    import numpy as np
    import concourse.bacc as bacc
    from concourse.bass_utils import run_bass_kernel_spmd

    nc = bacc.Bacc("TRN2", target_bir_lowering=False, num_devices=1)
    given = {name: np.ascontiguousarray(inputs[name]) for name in INPUTS}
    given.update(shape_constants(given["L0_xattn_igate_b"].shape[0]))
    arrays, args = {}, []
    for name, a in given.items():
        arrays[f"in_{name}"] = a
        args.append(nc.dram_tensor(f"in_{name}", a.shape, mybir.dt.from_np(a.dtype), kind="ExternalInput").ap())
    args.append(nc.dram_tensor("out_0", given["x"].shape, mybir.dt.float32, kind="ExternalOutput").ap())
    build_kernel(nc, *args)
    r = run_bass_kernel_spmd(nc, [arrays], core_ids=[0])
    return r.results[0]["out_0"]
```

```python
import math
from contextlib import ExitStack

import concourse.bass as bass
from concourse import mybir

P = 128
GROUP = 4
RING = 8


ROUNDING = "scaled exponent magic up down size past nan out"


class Batch:

    def __init__(self, it, k):
        self.it, self.k = it, k

    def __add__(self, d):
        return Batch(self.it, self.k + d)

    def __sub__(self, d):
        return Batch(self.it, self.k - d)

    @property
    def known(self):
        return isinstance(self.it, int)

    @property
    def index(self):
        return self.it * RING + self.k

    def exists(self, batches):
        return not self.known or 0 <= self.index < batches

    def follows(self, batches):
        return not self.known or self.index >= batches

    def count(self, each, done, unit=1):
        return self.it * (each * RING // unit) + each * (self.k // unit) + done


class Stage:

    def __init__(self, sem, steps, unit=1):
        self.sem, self.steps, self.unit = sem, steps.split(), unit

    def at(self, batch, step):
        return batch.count(len(self.steps), self.steps.index(step) + 1, self.unit)


def build_kernel(nc, x, ctx, igate_w, igate_b, fgate_w, fgate_b, out_w, ffn_w, s_in, s_k, bias,
                 c_ident, c_gsel, c_hsel, out):
    f32, bf16, fp8, i32 = mybir.dt.float32, mybir.dt.bfloat16, mybir.dt.float8e4, mybir.dt.int32
    ALU, ACT, AX = mybir.AluOpType, mybir.ActivationFunctionType, mybir.AxisListType
    B, S, E = x.shape
    NH = igate_b.shape[0]
    DH = E // NH
    T = S // P
    C = E // P
    F = ffn_w.shape[1]
    R = GROUP * NH
    U = 2
    W = DH + 1
    EPS, LN_EPS = 1e-6, 1e-5
    Q_SCALE = DH ** -0.5
    TOP = 1e17
    WIDE_PIECES = C * S // P
    assert (T, C, U, DH) == (2, 4, 2, 64) and B % RING == 0 and B >= 3 * RING

    es = ExitStack()
    with es:
        def sb(name, shape, dt=f32):
            return es.enter_context(nc.sbuf_tensor(name, shape, dt))

        def sem(name):
            return es.enter_context(nc.semaphore(name))

        x_sb = sb("x_sb", [P, RING, T, E])
        c_sb = sb("c_sb", [P, RING, T, E])
        qT = sb("qT", [P, RING, C, S])
        kT = sb("kT", [P, RING, C, S])
        val = sb("val", [P, 2, T * NH, W])
        g_sb = sb("g_sb", [P, 2, T * NH, W])
        x1 = sb("x1", [P, 2, T, E])
        q_nat = sb("q_nat", [P, T, E])
        bn1 = sb("bn1", [P, T, 6])
        mv1 = sb("mv1", [P, T, 2])
        log1 = sb("log1", [P, T])
        r1 = sb("r1", [P, T])
        nb1 = sb("nb1", [P, T])
        g_part = sb("g_part", [P, GROUP, S])
        z_abs = sb("z_abs", [R, S])
        ncs = sb("ncs", [R, S])
        am = sb("am", [R, 2 * S])
        mx = sb("mx", [R, S])
        ex = sb("ex", [R, 2 * S])
        z_f, z_neg = ex[:, 0:S], ex[:, S:2 * S]
        scratch = sb("scratch", [P, 2 * S])
        rest = scratch[0:R, :]
        part2 = sb("part2", [R, 2 * S], bf16)
        split = sb("split", [P, 2, 2 * S], bf16)
        facs = sb("facs", [P, 2, 4, R])
        v_sum = sb("v_sum", [P, T * NH])
        v_mean = sb("v_mean", [P, T * NH])
        k_w = sb("k_w", [P, E])
        dec = sb("dec", [P, 4, 4 * P])
        state = sb("state", [P, U, 2, 2 * W])
        carry = sb("carry", [P, NH, W])
        g_ss = sb("g_ss", [P, T * NH])
        h_n0 = sb("h_n0", [P, T, NH])
        h_n = sb("h_n", [P, T, NH])
        h_n2 = sb("h_n2", [P, T * NH])
        h_v = sb("h_v", [P, T * NH])
        h_log = sb("h_log", [P, T * NH])
        h_r = sb("h_r", [P, T * NH])
        bn2 = sb("bn2", [P, T, 6])
        mv2 = sb("mv2", [P, T, 2])
        log2 = sb("log2", [P, T])
        r2 = sb("r2", [P, T])
        nb2 = sb("nb2", [P, T])
        z_bf = sb("z_bf", [P, T, E], bf16)
        zq = sb("zq", [P, C, S], fp8)
        zq_wide = z_bf[:, :, :].rearrange("p t e -> p (t e)").rearrange("p (c s) -> p c s", c=C)
        wide_val, wide_mag, wide_tmp = (scratch[:, i * P:(i + 1) * P] for i in range(3))
        y_bf = sb("y_bf", [P, T, F], bf16)
        o_sb = sb("o_sb", [P, T, F])
        ident = sb("ident", [P, P])
        ident_bf = sb("ident_bf", [P, P], bf16)
        gsel = sb("gsel", [P, GROUP, 2 * R])
        hsel_f = sb("hsel_f", [P, R])
        hsel = sb("hsel", [P, R], bf16)
        w_x = sb("w_x", [P, C, 32])
        w_c = sb("w_c", [P, C, 32])
        b_i = sb("b_i", [R, 1])
        b_f = sb("b_f", [R, 1])
        w_out = sb("w_out", [P, E])
        w_ffn = sb("w_ffn", [P, C, F], bf16)
        b_ffn = sb("b_ffn", [P, F], bf16)
        sc = sb("sc", [P, 2])
        s_inv = sb("s_inv", [P, 2])
        s_out = sb("s_out", [P, 1])
        s_abs = sb("s_abs", [P, 1])
        wide = sb("wide", [P, 1])
        ln_eps = sb("ln_eps", [P, 1])
        n_eps = sb("n_eps", [P, 1])
        ln_qs = sb("ln_qs", [P, 1])
        w_rows = x1[0:2 * NH, :, :, :].rearrange("p a t e -> p (a t e)")[:, 0:3 * E]
        f_val, f_mag, f_tmp = (dec[:, i, :] for i in range(3))

        bank = [es.enter_context(nc.psum_tensor(f"bank{i}", [P, 512], f32)) for i in range(8)]
        turn_ps = bank[0:2]
        gate_ps, arg_ps, qk_ps = bank[2], bank[3], bank[4]
        work_ps = bank[5:7]
        y_ps = bank[7]
        part_ps = gate_ps[:, 0:S]
        rows_ps = gate_ps[0:2 * R, S:2 * S]
        facs_ps = gate_ps[:, S:S + 4 * R]
        zt_ps = y_ps[:, :].bitcast(bf16)

        x_in = [sem(f"x_in{r}") for r in range(RING)]
        c_in = [sem(f"c_in{r}") for r in range(RING)]
        stored = sem("stored")
        consts_in, rows_in, ffn_in = sem("consts_in"), sem("rows_in"), sem("ffn_in")
        pool_set, gate_w_turned, dve_set = sem("pool_set"), sem("gate_w_turned"), sem("dve_set")
        v_norm = Stage(sem("v_norm"), "bn0 bn1 mv0 mv1 nb")
        a_norm = Stage(sem("a_norm"), "log r q0 q1")
        t_turn = Stage(sem("t_turn"), "r0 r1 r2 r3 gates")
        a_turn = Stage(sem("a_turn"), "r0 r1 r2 r3 gates")
        t_scan = Stage(sem("t_scan"), "rows turned", GROUP)
        v_scan = Stage(sem("v_scan"), "z neg abs ncs a m ex0 ex1 ex2 negm p1 rest p2 p2b p3", GROUP)
        a_scan = Stage(sem("a_scan"), "exp log ex facs", GROUP)
        v_val = Stage(sem("v_val"), "sum mean")
        p_val = Stage(sem("p_val"), "val0 val1")
        t_first = Stage(sem("t_first"), "arg0")
        t_attn = Stage(sem("t_attn"), "arg1 qk0 arg2 qk1 st0 st1 arg3 qk2 pv0 pv1 qk3 in0 in1 pv2")
        t_last = Stage(sem("t_last"), "pv3")
        a_first = Stage(sem("a_first"), "exp0")
        a_attn = Stage(sem("a_attn"), "exp1 exp2 st0 st1 exp3 g0 g1")
        p_attn = Stage(sem("p_attn"), "kw mask0 mask1 mask2 mask3")
        v_attn = Stage(sem("v_attn"), "c0 c1 c2 in0 in1 c3 g2")
        v_last = Stage(sem("v_last"), "g3")
        a_mix = Stage(sem("a_mix"), "sq n2 hlog hr log r z0 z1")
        v_mix = Stage(sem("v_mix"), "n0 n ss v hn x1 bn0 bn1 mv0 mv1 nb")
        p_mix = Stage(sem("p_mix"), "hw")
        t_ffn = Stage(sem("t_ffn"), "zt y0 y1")
        a_ffn = Stage(sem("a_ffn"), "zq y0 y1")
        v_ffn = Stage(sem("v_ffn"), "yb")
        v_wide = Stage(sem("v_wide"), " ".join(f"{step}{i}" for i in range(WIDE_PIECES) for step in
                                               ROUNDING.split()))
        p_ffn = Stage(sem("p_ffn"), "out0 out1")

        block = es.enter_context(nc.Block())

        def slots(eng, slot, *mode):
            for k in range(-5, RING):
                slot(Batch(0, k), *mode)
            with eng.Fori(1, B // RING - 1) as it:
                for k in range(RING):
                    slot(Batch(it, k), *mode)
            for k in range(RING + 3):
                slot(Batch(B // RING - 1, k), *mode)

        def slots_by_range(eng, slot):
            with eng.If(eng.value_load(wide[0:1, 0:1].bitcast(i32)) > 0):
                slots(eng, slot, True)
            with eng.Else():
                slots(eng, slot, False)

        def scans(m):
            return (m + 1).k % GROUP == 0 and (m + 1).exists(B)

        def heads(ap):
            return ap.rearrange("p (h d) -> p h d", d=DH)

        N_CONSTS = 16 * (3 + 2 * GROUP + 2)
        N_POOL_SET, N_DVE_SET = 5, 12 + len(ROUNDING.split()) * C

        @block.sync
        def _(sp):
            def rows_of(t, b):
                return t[bass.ds(b.index, 1), :, :].rearrange("o (t p) e -> p (o t) e", p=P)

            def load(b):
                r = b.k % RING
                if b.follows(RING):
                    sp.wait_ge(v_mix.sem, v_mix.at(b - RING, "x1"))
                sp.dma_start(x_sb[:, r, :, :], rows_of(x, b)).then_inc(x_in[r], 16)
                if b.follows(RING):
                    sp.wait_ge(p_attn.sem, p_attn.at(b - RING, "kw"))
                sp.dma_start(c_sb[:, r, :, :], rows_of(ctx, b)).then_inc(c_in[r], 16)

            sp.dma_start(ident[:, :], c_ident).then_inc(consts_in, 16)
            sp.dma_start(w_rows[0:NH, :], igate_w).then_inc(rows_in, 16)
            sp.dma_start(w_rows[NH:2 * NH, :], fgate_w).then_inc(rows_in, 16)
            sp.dma_start(w_ffn[:, :, :], ffn_w.rearrange("(c p) f -> p c f", p=P)).then_inc(ffn_in, 16)
            for col, s in ((0, s_in), (1, s_k)):
                sp.dma_start(sc[:, col:col + 1], s.partition_broadcast(P)).then_inc(ffn_in, 16)
            load(Batch(0, 0))
            load(Batch(0, 1))
            sp.dma_start(gsel[:, :, :], c_gsel).then_inc(consts_in, 16)
            sp.dma_start(hsel_f[:, :], c_hsel).then_inc(consts_in, 16)
            for j in range(GROUP):
                for dst, src in ((b_i, igate_b), (b_f, fgate_b)):
                    sp.dma_start(dst[j * NH:(j + 1) * NH, :],
                                 src.rearrange("(h o) -> h o", o=1)).then_inc(consts_in, 16)
            sp.dma_start(w_out[:, :], out_w.partition_broadcast(P)).then_inc(consts_in, 16)
            sp.dma_start(b_ffn[:, :], bias.partition_broadcast(P)).then_inc(consts_in, 16)

            def slot(m):
                if (m - 3).exists(B):
                    sp.wait_ge(p_ffn.sem, p_ffn.at(m - 3, "out1"))
                    sp.dma_start(rows_of(out, m - 3), o_sb[:, :, :]).then_inc(stored, 16)
                if (m + 7).exists(B):
                    load(m + 7)

            slots(sp, slot)
            sp.wait_ge(stored, 16 * B)

        @block.tensor
        def _(pe):
            mm, turn = nc.tensor.matmul, nc.tensor.transpose

            pe.wait_ge(consts_in, N_CONSTS)
            pe.wait_ge(rows_in, 32)
            for i in range(3 * C):
                last = turn(gate_ps[:, i * 2 * NH:(i + 1) * 2 * NH], w_rows[:, i * P:(i + 1) * P],
                            ident[0:2 * NH, 0:2 * NH])
            last.then_inc(gate_w_turned, 1)
            pe.wait_ge(dve_set, N_DVE_SET)
            pe.wait_ge(pool_set, N_POOL_SET)

            def turn_round(b, i):
                if i == 0:
                    pe.wait_ge(a_norm.sem, a_norm.at(b, "q1"))
                if i == 2:
                    pe.wait_ge(c_in[b.k % RING], b.count(16, 16, RING))
                if i >= 2:
                    pe.wait_ge(a_turn.sem, a_turn.at(b, f"r{i - 2}"))
                elif b.follows(1):
                    pe.wait_ge(a_turn.sem, a_turn.at(b - 1, f"r{i + 2}"))
                for c in range(2):
                    for t in range(T):
                        chunk = slice((2 * (i % 2) + c) * P, (2 * (i % 2) + c + 1) * P)
                        src = q_nat[:, t, chunk] if i < 2 else c_sb[:, b.k % RING, t, chunk]
                        last = turn(turn_ps[i % 2][:, (T * c + t) * P:(T * c + t + 1) * P], src, ident[:, :])
                last.then_inc(t_turn.sem, 1)

            def gates(b):
                r = b.k % RING
                pe.wait_ge(a_turn.sem, a_turn.at(b, "r3"))
                if b.follows(1):
                    pe.wait_ge(a_turn.sem, a_turn.at(b - 1, "gates"))
                for w, src, first in ((w_x, qT, True), (w_c, kT, False)):
                    for c in range(C):
                        last = mm(part_ps[32 * c:32 * c + 32, :], w[:, c, :], src[:, r, c, :],
                                  start=first, stop=not first)
                last.then_inc(t_turn.sem, 1)

            def scan_rows(b):
                pe.wait_ge(a_turn.sem, a_turn.at(b + (GROUP - 1), "gates"))
                if b.follows(GROUP):
                    pe.wait_ge(a_scan.sem, a_scan.at(b - GROUP, "facs"))
                for j in range(GROUP):
                    last = mm(rows_ps, gsel[:, j, :], g_part[:, j, :], start=j == 0, stop=j == GROUP - 1)
                last.then_inc(t_scan.sem, 1)

            def scan_turned(b):
                for i in range(4):
                    last = turn(facs_ps[:, i * R:(i + 1) * R], ex[:, i * P:(i + 1) * P], ident[0:R, 0:R])
                last.then_inc(t_scan.sem, 1)

            def arg(b, q):
                t, u, j, g = q // U, q % U, b.k % GROUP, b.k // GROUP % 2
                row = j * NH + u
                if q == 0:
                    pe.wait_ge(v_scan.sem, v_scan.at(b, "p3"))
                if q == 1:
                    pe.wait_ge(a_first.sem, a_first.at(b, "exp0"))
                elif q:
                    pe.wait_ge(a_attn.sem, a_attn.at(b, f"exp{q - 1}"))
                elif b.follows(1):
                    pe.wait_ge(a_attn.sem, a_attn.at(b - 1, "exp3"))
                mm(arg_ps[:, :], split[:, g, t * P:(t + 1) * P], hsel[:, row:row + NH - 1:2].unsqueeze(2).broadcast_to([P, 4, P]),
                   start=True, stop=False)
                for h in range(4):
                    last = mm(arg_ps[:, h * P:(h + 1) * P], hsel[:, row + 2 * h:row + 2 * h + 1].broadcast_to([P, P]),
                              split[:, g, S + t * P:S + (t + 1) * P], start=False, stop=h == 3)
                last.then_inc((t_attn if q else t_first).sem, 1)

            def scores(b, q):
                t, u, r = q // U, q % U, b.k % RING
                if q:
                    pe.wait_ge(v_attn.sem, v_attn.at(b, f"c{q - 1}"))
                elif b.follows(1):
                    pe.wait_ge(v_attn.sem, v_attn.at(b - 1, "c3"))
                half = slice(DH * u, DH * u + DH)
                for c in range(C):
                    last = mm(qk_ps[:, c * P:(c + 1) * P], kT[half, r, c, t * P:(t + 1) * P],
                              qT[half, r, c, t * P:(t + 1) * P], start=True, stop=True)
                last.then_inc(t_attn.sem, 1)

            def states(b, u):
                if u == 0:
                    pe.wait_ge(p_attn.sem, p_attn.at(b, "kw"))
                    pe.wait_ge(p_val.sem, p_val.at(b, "val1"))
                if b.follows(1) and u == 0:
                    pe.wait_ge(v_attn.sem, v_attn.at(b - 1, "g2"))
                elif b.follows(1):
                    pe.wait_ge(v_last.sem, v_last.at(b - 1, "g3"))
                for i in range(2):
                    pair = 2 * u + i
                    last = mm(work_ps[u][:, i * 2 * W:(i + 1) * 2 * W], k_w[:, pair * P:(pair + 1) * P],
                              val[:, b.k % 2, 2 * pair:2 * pair + 2, :], start=True, stop=True)
                last.then_inc(t_attn.sem, 1)

            def within(b, q):
                t, u = q // U, q % U
                pe.wait_ge(v_attn.sem, v_attn.at(b, ("c0", "c1", "in0", "c3")[q]))
                if t == 0:
                    pe.wait_ge(a_attn.sem, a_attn.at(b, f"st{u}"))
                for h in range(4):
                    last = mm(work_ps[u][:, h * W:(h + 1) * W], dec[:, q, h * P:(h + 1) * P],
                              val[:, b.k % 2, t * NH + 2 * h + u, :], start=True, stop=True)
                last.then_inc((t_attn if q < 3 else t_last).sem, 1)

            def across(b, u):
                pe.wait_ge(a_attn.sem, a_attn.at(b, f"g{u}"))
                for i in range(2):
                    last = mm(work_ps[u][:, i * 2 * W:(i + 1) * 2 * W], qT[:, b.k % RING, 2 * u + i, P:2 * P],
                              state[:, u, i, :], start=True, stop=True)
                last.then_inc(t_attn.sem, 1)

            def ffn_turn(b):
                pe.wait_ge(a_mix.sem, a_mix.at(b, "z1"))
                if b.follows(1):
                    pe.wait_ge(a_ffn.sem, a_ffn.at(b - 1, "y1"))
                for c in range(C):
                    for t in range(T):
                        last = turn(zt_ps[:, c * S + t * P:c * S + (t + 1) * P],
                                    z_bf[:, t, c * P:(c + 1) * P], ident_bf[:, :])
                last.then_inc(t_ffn.sem, 1)

            def ffn(b, t, wide_z):
                if wide_z and t == 0:
                    pe.wait_ge(v_wide.sem, v_wide.at(b, f"out{WIDE_PIECES - 1}"))
                for c in range(C):
                    last = mm(y_ps[:, :], (zq_wide if wide_z else zq)[:, c, t * P:(t + 1) * P],
                              w_ffn[:, c, :], start=c == 0, stop=c == C - 1)
                last.then_inc(t_ffn.sem, 1)

            def slot(m, wide_z):
                turning, opening, attending, closing, feeding = ((m + d).exists(B) for d in (4, 1, 0, -1, -2))
                if turning:
                    turn_round(m + 4, 0)
                if attending:
                    arg(m, 1)
                if turning:
                    turn_round(m + 4, 1)
                if attending:
                    scores(m, 0)
                if turning:
                    turn_round(m + 4, 2)
                if closing:
                    within(m - 1, 3)
                if turning:
                    turn_round(m + 4, 3)
                if attending:
                    arg(m, 2)
                    scores(m, 1)
                if feeding:
                    ffn_turn(m - 2)
                if turning:
                    gates(m + 4)
                if attending:
                    states(m, 0)
                    states(m, 1)
                    arg(m, 3)
                if scans(m):
                    scan_rows(m + 1)
                if feeding:
                    pe.wait_ge(a_ffn.sem, a_ffn.at(m - 2, "zq"))
                if attending:
                    scores(m, 2)
                if feeding:
                    ffn(m - 2, 0, wide_z)
                if attending:
                    within(m, 0)
                    within(m, 1)
                    scores(m, 3)
                if feeding:
                    pe.wait_ge(a_ffn.sem, a_ffn.at(m - 2, "y0"))
                if attending:
                    across(m, 0)
                if scans(m):
                    pe.wait_ge(a_scan.sem, a_scan.at(m + 1, "ex"))
                if attending:
                    across(m, 1)
                if feeding:
                    ffn(m - 2, 1, wide_z)
                if opening:
                    arg(m + 1, 0)
                if scans(m):
                    scan_turned(m + 1)
                if attending:
                    within(m, 2)

            slots_by_range(pe, slot)

        @block.scalar
        def _(act):
            af = nc.scalar.activation
            nc.scalar.preload_act_table_set("natural_log_exp_and_others")
            act.wait_ge(dve_set, N_DVE_SET)
            act.wait_ge(pool_set, N_POOL_SET)

            def turned(b, i):
                act.wait_ge(t_turn.sem, t_turn.at(b, f"r{i}"))
                dst = (qT if i < 2 else kT)[:, b.k % RING, 2 * (i % 2):2 * (i % 2) + 2, :]
                af(dst.rearrange("p c s -> p (c s)"), turn_ps[i % 2][:, :], ACT.Copy).then_inc(a_turn.sem, 1)

            def gates(b):
                act.wait_ge(t_turn.sem, t_turn.at(b, "gates"))
                af(g_part[:, b.k % GROUP, :], part_ps, ACT.Copy).then_inc(a_turn.sem, 1)

            def decay(b, q):
                if q == 0:
                    act.wait_ge(t_first.sem, t_first.at(b, "arg0"))
                else:
                    act.wait_ge(t_attn.sem, t_attn.at(b, f"arg{q}"))
                af(dec[:, q, :], arg_ps[:, :], ACT.Exp).then_inc((a_attn if q else a_first).sem, 1)

            def keep_states(b):
                for u in range(U):
                    act.wait_ge(t_attn.sem, t_attn.at(b, f"st{u}"))
                    src = work_ps[u][:, 0:4 * W].rearrange("p (i w) -> p i w", i=2)
                    af(state[0:DH, u, :, 0:W], src[0:DH, :, 0:W], ACT.Copy)
                    af(state[DH:P, u, :, W:2 * W], src[DH:P, :, W:2 * W], ACT.Copy).then_inc(a_attn.sem, 1)

            def keep_tile0(b, u):
                act.wait_ge(t_attn.sem, t_attn.at(b, f"pv{u}"))
                if b.follows(2):
                    act.wait_ge(v_mix.sem, v_mix.at(b - 2, "hn"))
                af(g_sb[:, b.k % 2, u:NH:2, :], work_ps[u][:, 0:4 * W].rearrange("p (h w) -> p h w", w=W),
                   ACT.Copy).then_inc(a_attn.sem, 1)

            def norm_rstd(b):
                act.wait_ge(v_norm.sem, v_norm.at(b, "mv1"))
                af(log1[:, :], mv1[:, :, 1], ACT.Ln, bias=ln_eps[:, :]).then_inc(a_norm.sem, 1)
                act.wait_ge(a_norm.sem, a_norm.at(b, "log"))
                af(r1[:, :], log1[:, :], ACT.Exp, scale=-0.5, bias=ln_qs[:, :]).then_inc(a_norm.sem, 1)

            def norm_apply(b, t):
                if t == 0:
                    act.wait_ge(v_norm.sem, v_norm.at(b, "nb"))
                    if b.follows(1):
                        act.wait_ge(t_turn.sem, t_turn.at(b - 1, "r1"))
                af(q_nat[:, t, :], x_sb[:, b.k % RING, t, :], ACT.Identity, bias=nb1[:, t:t + 1],
                   scale=r1[:, t:t + 1]).then_inc(a_norm.sem, 1)

            def scan_softplus(b):
                act.wait_ge(v_scan.sem, v_scan.at(b, "abs"))
                af(z_abs[:, :], z_abs[:, :], ACT.Exp, scale=-1.0).then_inc(a_scan.sem, 1)
                act.wait_ge(a_scan.sem, a_scan.at(b, "exp"))
                af(z_abs[:, :], z_abs[:, :], ACT.Ln, bias=1.0).then_inc(a_scan.sem, 1)

            def scan_exps(b):
                act.wait_ge(v_scan.sem, v_scan.at(b, "ex2"))
                af(ex[:, :], ex[:, :], ACT.Exp).then_inc(a_scan.sem, 1)

            def scan_facs(b):
                act.wait_ge(t_scan.sem, t_scan.at(b, "turned"))
                af(facs[:, b.k // GROUP % 2, :, :].rearrange("p k r -> p (k r)"), facs_ps,
                   ACT.Copy).then_inc(a_scan.sem, 1)

            def squares(b):
                act.wait_ge(v_last.sem, v_last.at(b, "g3"))
                act.wait_ge(a_attn.sem, a_attn.at(b, "g1"))
                if b.follows(2):
                    act.wait_ge(p_ffn.sem, p_ffn.at(b - 2, "out1"))
                af(x1[:, b.k % 2, :, :].rearrange("p t (h d) -> p (t h) d", d=DH),
                   g_sb[:, b.k % 2, :, 0:DH], ACT.Square).then_inc(a_mix.sem, 1)

            def normaliser_square(b):
                act.wait_ge(v_mix.sem, v_mix.at(b, "n"))
                af(h_n2[:, :], h_n[:, :, :].rearrange("p t h -> p (t h)"), ACT.Square,
                   bias=n_eps[:, :]).then_inc(a_mix.sem, 1)

            def head_rstd(b):
                act.wait_ge(v_mix.sem, v_mix.at(b, "v"))
                af(h_log[:, :], h_v[:, :], ACT.Ln, scale=1.0 / DH).then_inc(a_mix.sem, 1)
                act.wait_ge(a_mix.sem, a_mix.at(b, "hlog"))
                af(h_r[:, :], h_log[:, :], ACT.Exp, scale=-0.5).then_inc(a_mix.sem, 1)

            def mix_rstd(b):
                act.wait_ge(v_mix.sem, v_mix.at(b, "mv1"))
                af(log2[:, :], mv2[:, :, 1], ACT.Ln, bias=ln_eps[:, :]).then_inc(a_mix.sem, 1)
                act.wait_ge(a_mix.sem, a_mix.at(b, "log"))
                af(r2[:, :], log2[:, :], ACT.Exp, scale=-0.5).then_inc(a_mix.sem, 1)

            def mix_apply(b, t):
                if t == 0:
                    act.wait_ge(v_mix.sem, v_mix.at(b, "nb"))
                    if b.follows(1):
                        act.wait_ge(t_ffn.sem, t_ffn.at(b - 1, "zt"))
                af(z_bf[:, t, :], x1[:, b.k % 2, t, :], ACT.Identity, bias=nb2[:, t:t + 1],
                   scale=r2[:, t:t + 1]).then_inc(a_mix.sem, 1)

            def quantise(b):
                af(zq[:, :, :].rearrange("p c s -> p (c s)"), zt_ps, ACT.Copy, scale=s_inv[:, 0:1],
                   saturate=False).then_inc(a_ffn.sem, 1)

            def dequantise(b, t):
                act.wait_ge(t_ffn.sem, t_ffn.at(b, f"y{t}"))
                if t == 0:
                    if b.follows(1):
                        act.wait_ge(p_ffn.sem, p_ffn.at(b - 1, "out1"))
                af(y_bf[:, t, :], y_ps[:, :], ACT.Copy, scale=s_out[:, :]).then_inc(a_ffn.sem, 1)

            def slot(m):
                norming, turning, opening, attending, mixing, feeding = (
                    (m + d).exists(B) for d in (5, 4, 1, 0, -1, -2))
                if turning:
                    turned(m + 4, 0)
                if feeding:
                    mix_rstd(m - 2)
                if attending:
                    decay(m, 1)
                if turning:
                    turned(m + 4, 1)
                if feeding:
                    mix_apply(m - 2, 0)
                if turning:
                    turned(m + 4, 2)
                if feeding:
                    mix_apply(m - 2, 1)
                if turning:
                    turned(m + 4, 3)
                if attending:
                    decay(m, 2)
                if mixing:
                    squares(m - 1)
                if feeding:
                    act.wait_ge(t_ffn.sem, t_ffn.at(m - 2, "zt"))
                if mixing:
                    normaliser_square(m - 1)
                if feeding:
                    quantise(m - 2)
                if turning:
                    gates(m + 4)
                if attending:
                    keep_states(m)
                if norming:
                    norm_rstd(m + 5)
                if mixing:
                    head_rstd(m - 1)
                if scans(m):
                    scan_softplus(m + 1)
                if attending:
                    decay(m, 3)
                    keep_tile0(m, 0)
                if feeding:
                    dequantise(m - 2, 0)
                if attending:
                    keep_tile0(m, 1)
                if scans(m):
                    scan_exps(m + 1)
                if norming:
                    norm_apply(m + 5, 0)
                    norm_apply(m + 5, 1)
                if feeding:
                    dequantise(m - 2, 1)
                if opening:
                    decay(m + 1, 0)
                if scans(m):
                    scan_facs(m + 1)

            slots(act, slot)

        @block.vector
        def _(dve):
            ve = nc.vector
            tt, ts, stt = ve.tensor_tensor, ve.tensor_scalar, ve.scalar_tensor_tensor
            done = [0]

            def setup(ins):
                done[0] += 1
                ins.then_inc(dve_set, 1)
                dve.wait_ge(dve_set, done[0])

            dve.wait_ge(pool_set, N_POOL_SET)
            setup(ve.memset(ln_eps[:, :], LN_EPS))
            setup(ve.memset(n_eps[:, :], EPS))
            setup(ve.memset(ln_qs[:, :], math.log(Q_SCALE)))
            dve.wait_ge(consts_in, N_CONSTS)
            setup(ve.tensor_copy(ident_bf[:, :], ident[:, :]))
            setup(ve.tensor_copy(hsel[:, :], hsel_f[:, :]))
            dve.wait_ge(gate_w_turned, 1)
            turned = gate_ps[:, 0:3 * C * 2 * NH].rearrange("p (k c g) -> p k c g", k=3, c=C)
            setup(ts(w_x[:, :, 0:2 * NH], turned[:, 0, :, :], 1.0 / Q_SCALE, None, ALU.mult))
            setup(ve.tensor_copy(w_c[:, :, 0:2 * NH], turned[:, 1, :, :]))
            setup(tt(w_c[:, :, 0:2 * NH], turned[:, 2, :, :], w_c[:, :, 0:2 * NH], ALU.add))
            dve.wait_ge(ffn_in, 48)
            setup(ve.reciprocal(s_inv[:, :], sc[:, :]))
            setup(tt(s_out[:, :], sc[:, 0:1], sc[:, 1:2], ALU.mult))
            setup(stt(s_abs[:, :], sc[:, 0:1], -1.0, sc[:, 0:1], ALU.mult, ALU.max))
            setup(ts(wide[:, :], s_abs[:, :], 22.7 / 240, None, ALU.is_lt))

            def round_e4m3fn(out, src, scale, val, mag, tmp, step):
                step(ts(val, src, scale, None, ALU.mult))
                step(ts(mag.bitcast(i32), val.bitcast(i32), 0x7F800000, None, ALU.bitwise_and))
                step(ts(mag, mag, 2.0 ** -6, 1.5 * 2.0 ** 20, ALU.max, ALU.mult))
                step(tt(tmp, val, mag, ALU.add))
                step(tt(val, tmp, mag, ALU.subtract))
                step(stt(tmp, val, -1.0, val, ALU.mult, ALU.max))
                step(ts(tmp, tmp, 448.0, 3e38, ALU.is_gt, ALU.mult))
                step(ts(mag, tmp, 3e38, None, ALU.mult))
                step(stt(out, mag, 0.0, val, ALU.mult, ALU.add))

            for c in range(C):
                round_e4m3fn(w_ffn[:, c, :], w_ffn[:, c, :], s_inv[:, 1:2], f_val, f_mag, f_tmp, setup)
            assert done[0] == N_DVE_SET

            def norm_stats(b):
                r = b.k % RING
                dve.wait_ge(x_in[r], b.count(16, 16, RING))
                for t in range(T):
                    ve.bn_stats(bn1[:, t, :], x_sb[:, r, t, :]).then_inc(v_norm.sem, 1)

            def norm_moments(b):
                for t in range(T):
                    ve.bn_aggr(mv1[:, t, :], bn1[:, t, :]).then_inc(v_norm.sem, 1)

            def norm_scale(b):
                dve.wait_ge(a_norm.sem, a_norm.at(b, "r"))
                stt(nb1[:, :], mv1[:, :, 0], -1.0, r1[:, :], ALU.mult, ALU.mult).then_inc(v_norm.sem, 1)

            def value_means(b):
                r = b.k % RING
                dve.wait_ge(c_in[r], b.count(16, 16, RING))
                ve.tensor_reduce(v_sum[:, :], c_sb[:, r, :, :].rearrange("p t (h d) -> p (t h) d", d=DH),
                                 AX.X, ALU.add).then_inc(v_val.sem, 1)
                dve.wait_ge(v_val.sem, v_val.at(b, "sum"))
                if b.follows(1):
                    dve.wait_ge(p_val.sem, p_val.at(b - 1, "val1"))
                ts(v_mean[:, :], v_sum[:, :], 1.0 / DH, None, ALU.mult).then_inc(v_val.sem, 1)

            def matrix(b, q):
                dve.wait_ge(t_attn.sem, t_attn.at(b, f"qk{q}"))
                dve.wait_ge(p_attn.sem, p_attn.at(b, f"mask{q}"))
                tt(dec[:, q, :], qk_ps[:, :], dec[:, q, :], ALU.mult).then_inc(v_attn.sem, 1)

            def carried(b, u):
                row, g = b.k % GROUP * NH + 4 * u, b.k // GROUP % 2
                dve.wait_ge(t_attn.sem, t_attn.at(b, f"in{u}"))
                tt(carry[:, 4 * u:4 * u + 4, :], work_ps[u][:, 0:4 * W].rearrange("p (h w) -> p h w", w=W),
                   facs[:, g, 2, row:row + 4].unsqueeze(2).broadcast_to([P, 4, W]),
                   ALU.mult).then_inc(v_attn.sem, 1)

            def keep_tile1(b, u):
                if u == 0:
                    dve.wait_ge(t_attn.sem, t_attn.at(b, "pv2"))
                    dve.wait_ge(v_attn.sem, v_attn.at(b, "in1"))
                else:
                    dve.wait_ge(t_last.sem, t_last.at(b, "pv3"))
                tt(g_sb[:, b.k % 2, NH + u:2 * NH:2, :], work_ps[u][:, 0:4 * W].rearrange("p (h w) -> p h w", w=W),
                   carry[:, u:NH:2, :], ALU.add).then_inc((v_last if u else v_attn).sem, 1)

            def normaliser(b):
                dve.wait_ge(v_last.sem, v_last.at(b, "g3"))
                dve.wait_ge(a_attn.sem, a_attn.at(b, "g1"))
                row, g = b.k % GROUP * NH, b.k // GROUP % 2
                sums = g_sb[:, b.k % 2, :, DH].rearrange("p (t h) -> p t h", t=T)
                stt(h_n0[:, :, :], sums, -1.0, facs[:, g, 0:T, row:row + NH], ALU.mult,
                    ALU.max).then_inc(v_mix.sem, 1)
                dve.wait_ge(v_mix.sem, v_mix.at(b, "n0"))
                stt(h_n[:, :, :], h_n0[:, :, :], TOP, sums, ALU.min, ALU.max).then_inc(v_mix.sem, 1)

            def head_squares(b):
                dve.wait_ge(a_mix.sem, a_mix.at(b, "sq"))
                ve.tensor_reduce(g_ss[:, :], x1[:, b.k % 2, :, :].rearrange("p t (h d) -> p (t h) d", d=DH),
                                 AX.X, ALU.add).then_inc(v_mix.sem, 1)

            def head_var(b):
                dve.wait_ge(v_mix.sem, v_mix.at(b, "ss"))
                dve.wait_ge(a_mix.sem, a_mix.at(b, "n2"))
                stt(h_v[:, :], h_n2[:, :], LN_EPS * DH, g_ss[:, :], ALU.mult, ALU.add).then_inc(v_mix.sem, 1)

            def head_norm(b):
                dve.wait_ge(a_mix.sem, a_mix.at(b, "hr"))
                tt(x1[:, b.k % 2, :, :].rearrange("p t (h d) -> p (t h) d", d=DH), g_sb[:, b.k % 2, :, 0:DH],
                   h_r[:, :].unsqueeze(2).broadcast_to([P, T * NH, DH]), ALU.mult).then_inc(v_mix.sem, 1)

            def residual(b):
                dve.wait_ge(p_mix.sem, p_mix.at(b, "hw"))
                tt(x1[:, b.k % 2, :, :], x1[:, b.k % 2, :, :], x_sb[:, b.k % RING, :, :],
                   ALU.add).then_inc(v_mix.sem, 1)

            def mix_stats(b):
                dve.wait_ge(v_mix.sem, v_mix.at(b, "x1"))
                for t in range(T):
                    ve.bn_stats(bn2[:, t, :], x1[:, b.k % 2, t, :]).then_inc(v_mix.sem, 1)

            def mix_moments(b):
                for t in range(T):
                    ve.bn_aggr(mv2[:, t, :], bn2[:, t, :]).then_inc(v_mix.sem, 1)

            def mix_scale(b):
                dve.wait_ge(a_mix.sem, a_mix.at(b, "r"))
                stt(nb2[:, :], mv2[:, :, 0], -1.0, r2[:, :], ALU.mult, ALU.mult).then_inc(v_mix.sem, 1)

            def quantise_wide(b):
                pieces = zq_wide.rearrange("p c s -> p (c s)").rearrange("p (i n) -> p i n", i=WIDE_PIECES)
                turned = zt_ps.rearrange("p (i n) -> p i n", i=WIDE_PIECES)
                steps = [0]

                def step(ins):
                    steps[0] += 1
                    ins.then_inc(v_wide.sem, 1)
                    if steps[0] < len(v_wide.steps):
                        dve.wait_ge(v_wide.sem, b.count(len(v_wide.steps), steps[0]))

                dve.wait_ge(a_ffn.sem, a_ffn.at(b, "zq"))
                for i in range(WIDE_PIECES):
                    round_e4m3fn(pieces[:, i, :], turned[:, i, :], s_inv[:, 0:1], wide_val,
                                 wide_mag, wide_tmp, step)

            def add_bias(b):
                dve.wait_ge(a_ffn.sem, a_ffn.at(b, "y1"))
                tt(y_bf[:, :, :], y_bf[:, :, :], b_ffn[:, :].unsqueeze(1).broadcast_to([P, T, F]),
                   ALU.add).then_inc(v_ffn.sem, 1)

            def scan_gate(b):
                dve.wait_ge(t_scan.sem, t_scan.at(b, "rows"))
                ts(z_f, rows_ps[R:2 * R, :], b_f[:, :], None, ALU.add).then_inc(v_scan.sem, 1)
                dve.wait_ge(v_scan.sem, v_scan.at(b, "z"))
                ts(z_neg, z_f, -1.0, 0.0, ALU.mult, ALU.max).then_inc(v_scan.sem, 1)
                stt(z_abs[:, :], z_f, -1.0, z_f, ALU.mult, ALU.max).then_inc(v_scan.sem, 1)

            def scan_sums(b):
                dve.wait_ge(a_scan.sem, a_scan.at(b, "log"))
                ve.tensor_tensor_scan(ncs[:, :], z_abs[:, :], z_neg, 0.0, ALU.add,
                                      ALU.add).then_inc(v_scan.sem, 1)
                dve.wait_ge(v_scan.sem, v_scan.at(b, "ncs"))
                stt(am[:, 0:S], rows_ps[0:R, :], b_i[:, :], ncs[:, :], ALU.add, ALU.add).then_inc(v_scan.sem, 1)
                dve.wait_ge(v_scan.sem, v_scan.at(b, "a"))
                ve.tensor_tensor_scan(mx[:, :], am[:, 0:S], am[:, 0:S], -3.0e38, ALU.max,
                                      ALU.max).then_inc(v_scan.sem, 1)
                dve.wait_ge(v_scan.sem, v_scan.at(b, "m"))
                tt(ex[:, 0:S], ncs[:, :], mx[:, :], ALU.subtract).then_inc(v_scan.sem, 1)
                ts(ex[:, S:S + P], mx[:, P:S], -1.0, mx[:, P - 1:P], ALU.mult, ALU.add).then_inc(v_scan.sem, 1)
                ts(ex[:, S + P:2 * S], am[:, 0:P], mx[:, P - 1:P], None, ALU.subtract).then_inc(v_scan.sem, 1)

            def scan_split(b):
                g = b.k // GROUP % 2
                ts(am[:, S:2 * S], mx[:, :], -1.0, None, ALU.mult).then_inc(v_scan.sem, 1)
                dve.wait_ge(v_scan.sem, v_scan.at(b, "negm"))
                ve.tensor_copy(split[0:R, g, :], am[:, :]).then_inc(v_scan.sem, 1)
                dve.wait_ge(v_scan.sem, v_scan.at(b, "p1"))
                tt(rest, am[:, :], split[0:R, g, :], ALU.subtract).then_inc(v_scan.sem, 1)
                dve.wait_ge(v_scan.sem, v_scan.at(b, "rest"))
                ve.tensor_copy(part2[:, :], rest).then_inc(v_scan.sem, 1)
                dve.wait_ge(v_scan.sem, v_scan.at(b, "p2"))
                ve.tensor_copy(split[R:2 * R, g, :], part2[:, :]).then_inc(v_scan.sem, 1)
                tt(split[2 * R:3 * R, g, :], rest, part2[:, :], ALU.subtract).then_inc(v_scan.sem, 1)

            def slot(m, wide_z):
                norming, valuing, attending, mixing, feeding, leaving = (
                    (m + d).exists(B) for d in (5, 1, 0, -1, -2, -3))
                if leaving:
                    add_bias(m - 3)
                if feeding:
                    mix_scale(m - 2)
                if attending:
                    matrix(m, 0)
                if valuing:
                    value_means(m + 1)
                if mixing:
                    keep_tile1(m - 1, 1)
                if norming:
                    norm_stats(m + 5)
                if mixing:
                    normaliser(m - 1)
                if norming:
                    dve.wait_ge(v_norm.sem, v_norm.at(m + 5, "bn1"))
                if attending:
                    matrix(m, 1)
                if feeding and wide_z:
                    quantise_wide(m - 2)
                if norming:
                    norm_moments(m + 5)
                if mixing:
                    head_squares(m - 1)
                    head_var(m - 1)
                if scans(m):
                    scan_gate(m + 1)
                if mixing:
                    head_norm(m - 1)
                if norming:
                    norm_scale(m + 5)
                if attending:
                    matrix(m, 2)
                if scans(m):
                    scan_sums(m + 1)
                if attending:
                    carried(m, 0)
                if scans(m):
                    scan_split(m + 1)
                if mixing:
                    residual(m - 1)
                    mix_stats(m - 1)
                if attending:
                    carried(m, 1)
                if mixing:
                    dve.wait_ge(v_mix.sem, v_mix.at(m - 1, "bn1"))
                if attending:
                    matrix(m, 3)
                if mixing:
                    mix_moments(m - 1)
                if attending:
                    keep_tile1(m, 0)

            slots_by_range(dve, slot)

        @block.gpsimd
        def _(pool):
            pl = nc.gpsimd
            pl.memset(val[:, :, :, DH:W], 1.0).then_inc(pool_set, 1)
            pl.memset(state[:, :, :, :], 0.0).then_inc(pool_set, 1)
            pl.memset(w_x[:, :, :], 0.0).then_inc(pool_set, 1)
            pl.memset(split[:, :, :], 0.0).then_inc(pool_set, 1)
            pl.memset(w_c[:, :, :], 0.0).then_inc(pool_set, 1)
            pool.wait_ge(consts_in, N_CONSTS)

            def weigh_keys(b):
                row, g = b.k % GROUP * NH, b.k // GROUP % 2
                pool.wait_ge(a_scan.sem, a_scan.at(b, "facs"))
                pool.wait_ge(c_in[b.k % RING], b.count(16, 16, RING))
                if b.follows(1):
                    pool.wait_ge(t_attn.sem, t_attn.at(b - 1, "st1"))
                pl.tensor_tensor(heads(k_w[:, :]), heads(c_sb[:, b.k % RING, 0, :]),
                                 facs[:, g, 3, row:row + NH].unsqueeze(2).broadcast_to([P, NH, DH]),
                                 ALU.mult).then_inc(p_attn.sem, 1)

            def mask(b, q):
                pl.affine_select(out=dec[:, q, :], in_=dec[:, q, :], compare_op=ALU.is_ge, fill=0.0, base=0,
                                 pattern=[[0, 4], [1, P]], channel_multiplier=-1).then_inc(p_attn.sem, 1)

            def scale_heads(b):
                pool.wait_ge(v_mix.sem, v_mix.at(b, "hn"))
                h = x1[:, b.k % 2, :, :]
                pl.tensor_tensor(h, h, w_out[:, :].unsqueeze(1).broadcast_to([P, T, E]),
                                 ALU.mult).then_inc(p_mix.sem, 1)

            def centre_values(b, t):
                if t == 0:
                    pool.wait_ge(v_val.sem, v_val.at(b, "mean"))
                    if b.follows(2):
                        pool.wait_ge(t_last.sem, t_last.at(b - 2, "pv3"))
                pl.tensor_tensor(val[:, b.k % 2, t * NH:(t + 1) * NH, 0:DH], heads(c_sb[:, b.k % RING, t, :]),
                                 v_mean[:, t * NH:(t + 1) * NH].unsqueeze(2).broadcast_to([P, NH, DH]),
                                 ALU.subtract).then_inc(p_val.sem, 1)

            def output(b, t):
                if t == 0:
                    pool.wait_ge(v_ffn.sem, v_ffn.at(b, "yb"))
                    if b.follows(1):
                        pool.wait_ge(stored, b.count(16, 0))
                pl.tensor_tensor(o_sb[:, t, :], x1[:, b.k % 2, t, :], y_bf[:, t, :],
                                 ALU.add).then_inc(p_ffn.sem, 1)

            def slot(m):
                valuing, attending, mixing, leaving = ((m + d).exists(B) for d in (1, 0, -1, -3))
                if attending:
                    pool.wait_ge(a_first.sem, a_first.at(m, "exp0"))
                    weigh_keys(m)
                    mask(m, 0)
                    pool.wait_ge(a_attn.sem, a_attn.at(m, "exp1"))
                if leaving:
                    output(m - 3, 0)
                    output(m - 3, 1)
                if attending:
                    mask(m, 1)
                if valuing:
                    centre_values(m + 1, 0)
                if attending:
                    pool.wait_ge(a_attn.sem, a_attn.at(m, "exp2"))
                if valuing:
                    centre_values(m + 1, 1)
                if attending:
                    mask(m, 2)
                    pool.wait_ge(a_attn.sem, a_attn.at(m, "exp3"))
                if mixing:
                    scale_heads(m - 1)
                if attending:
                    mask(m, 3)

            slots(pool, slot)


def shape_constants(n_heads):
    import numpy as np
    rows = GROUP * n_heads
    ident = np.eye(P, dtype=np.float32)
    gsel = np.zeros((P, GROUP, 2 * rows), np.float32)
    for chunk in range(P // 32):
        for j in range(GROUP):
            for h in range(n_heads):
                gsel[32 * chunk + h, j, j * n_heads + h] = 1
                gsel[32 * chunk + n_heads + h, j, rows + j * n_heads + h] = 1
    hsel = np.zeros((P, rows), np.float32)
    for part in range(3):
        for row in range(rows):
            hsel[part * rows + row, row] = 1
    return {"c_ident": ident, "c_gsel": gsel, "c_hsel": hsel}


INPUTS = ["x", "ctx_1024", "L0_xattn_igate_w", "L0_xattn_igate_b", "L0_xattn_fgate_w", "L0_xattn_fgate_b",
          "L0_xattn_out_w", "L0_ffn_kernel", "L0_ffn_input_scale", "L0_ffn_kernel_scale", "L0_ffn_bias"]


def kernel(**inputs):
    import numpy as np
    import concourse.bacc as bacc
    from concourse.bass_utils import run_bass_kernel_spmd

    nc = bacc.Bacc("TRN2", target_bir_lowering=False, num_devices=1)
    given = {name: np.ascontiguousarray(inputs[name]) for name in INPUTS}
    given.update(shape_constants(given["L0_xattn_igate_b"].shape[0]))
    arrays, args = {}, []
    for name, a in given.items():
        arrays[f"in_{name}"] = a
        args.append(nc.dram_tensor(f"in_{name}", a.shape, mybir.dt.from_np(a.dtype), kind="ExternalInput").ap())
    args.append(nc.dram_tensor("out_0", given["x"].shape, mybir.dt.float32, kind="ExternalOutput").ap())
    build_kernel(nc, *args)
    r = run_bass_kernel_spmd(nc, [arrays], core_ids=[0])
    return r.results[0]["out_0"]
```

```python
import math
from contextlib import ExitStack

import concourse.bass as bass
from concourse import mybir

P = 128
GROUP = 4
RING = 8


ROUNDING = "scaled exponent magic up down size past nan out"


class Batch:

    def __init__(self, it, k):
        self.it, self.k = it, k

    def __add__(self, d):
        return Batch(self.it, self.k + d)

    def __sub__(self, d):
        return Batch(self.it, self.k - d)

    @property
    def known(self):
        return isinstance(self.it, int)

    @property
    def index(self):
        return self.it * RING + self.k

    def exists(self, batches):
        return not self.known or 0 <= self.index < batches

    def follows(self, batches):
        return not self.known or self.index >= batches

    def count(self, each, done, unit=1):
        return self.it * (each * RING // unit) + each * (self.k // unit) + done


class Stage:

    def __init__(self, sem, steps, unit=1):
        self.sem, self.steps, self.unit = sem, steps.split(), unit

    def at(self, batch, step):
        return batch.count(len(self.steps), self.steps.index(step) + 1, self.unit)


def build_kernel(nc, x, ctx, igate_w, igate_b, fgate_w, fgate_b, out_w, ffn_w, s_in, s_k, bias,
                 c_ident, c_gsel, c_hsel, out):
    f32, bf16, fp8, i32 = mybir.dt.float32, mybir.dt.bfloat16, mybir.dt.float8e4, mybir.dt.int32
    ALU, ACT, AX = mybir.AluOpType, mybir.ActivationFunctionType, mybir.AxisListType
    B, S, E = x.shape
    NH = igate_b.shape[0]
    DH = E // NH
    T = S // P
    C = E // P
    F = ffn_w.shape[1]
    R = GROUP * NH
    U = 2
    W = DH + 1
    EPS, LN_EPS = 1e-6, 1e-5
    Q_SCALE = DH ** -0.5
    TOP = 1e17
    WIDE_PIECES = C * S // P
    assert (T, C, U, DH) == (2, 4, 2, 64) and B % RING == 0 and B >= 3 * RING

    es = ExitStack()
    with es:
        def sb(name, shape, dt=f32):
            return es.enter_context(nc.sbuf_tensor(name, shape, dt))

        def sem(name):
            return es.enter_context(nc.semaphore(name))

        x_sb = sb("x_sb", [P, RING, T, E])
        c_sb = sb("c_sb", [P, RING, T, E])
        qT = sb("qT", [P, RING, C, S])
        kT = sb("kT", [P, RING, C, S])
        val = sb("val", [P, 2, T * NH, W])
        g_sb = sb("g_sb", [P, 2, T * NH, W])
        x1 = sb("x1", [P, 2, T, E])
        q_nat = sb("q_nat", [P, T, E])
        bn1 = sb("bn1", [P, T, 6])
        mv1 = sb("mv1", [P, T, 2])
        log1 = sb("log1", [P, T])
        r1 = sb("r1", [P, T])
        nb1 = sb("nb1", [P, T])
        g_part = sb("g_part", [P, GROUP, S])
        z_abs = sb("z_abs", [R, S])
        ncs = sb("ncs", [R, S])
        am = sb("am", [R, 2 * S])
        mx = sb("mx", [R, S])
        ex = sb("ex", [R, 2 * S])
        z_f, z_neg = ex[:, 0:S], ex[:, S:2 * S]
        scratch = sb("scratch", [P, 2 * S])
        rest = scratch[0:R, :]
        part2 = sb("part2", [R, 2 * S], bf16)
        split = sb("split", [P, 2, 2 * S], bf16)
        facs = sb("facs", [P, 2, 4, R])
        v_sum = sb("v_sum", [P, T * NH])
        v_mean = sb("v_mean", [P, T * NH])
        k_w = sb("k_w", [P, E])
        dec = sb("dec", [P, 4, 4 * P])
        state = sb("state", [P, C, 2 * W])
        carry = sb("carry", [P, NH, W])
        g_ss = sb("g_ss", [P, T * NH])
        h_n0 = sb("h_n0", [P, T, NH])
        h_n = sb("h_n", [P, T, NH])
        h_n2 = sb("h_n2", [P, T * NH])
        h_v = sb("h_v", [P, T * NH])
        h_log = sb("h_log", [P, T * NH])
        h_r = sb("h_r", [P, T * NH])
        bn2 = sb("bn2", [P, T, 6])
        mv2 = sb("mv2", [P, T, 2])
        log2 = sb("log2", [P, T])
        r2 = sb("r2", [P, T])
        nb2 = sb("nb2", [P, T])
        z_bf = sb("z_bf", [P, T, E], bf16)
        zq = sb("zq", [P, C, S], fp8)
        zq_wide = z_bf[:, :, :].rearrange("p t e -> p (t e)").rearrange("p (c s) -> p c s", c=C)
        wide_val, wide_mag, wide_tmp = (scratch[:, i * P:(i + 1) * P] for i in range(3))
        y_bf = sb("y_bf", [P, T, F], bf16)
        o_sb = sb("o_sb", [P, T, F])
        ident = sb("ident", [P, P])
        ident_bf = sb("ident_bf", [P, P], bf16)
        gsel = sb("gsel", [P, GROUP, 2 * R])
        hsel_f = sb("hsel_f", [P, R])
        hsel = sb("hsel", [P, R], bf16)
        w_x = sb("w_x", [P, C, 32])
        w_c = sb("w_c", [P, C, 32])
        b_i = sb("b_i", [R, 1])
        b_f = sb("b_f", [R, 1])
        w_out = sb("w_out", [P, E])
        w_ffn = sb("w_ffn", [P, C, F], bf16)
        b_ffn = sb("b_ffn", [P, F], bf16)
        sc = sb("sc", [P, 2])
        s_inv = sb("s_inv", [P, 2])
        s_out = sb("s_out", [P, 1])
        s_abs = sb("s_abs", [P, 1])
        wide = sb("wide", [P, 1])
        ln_eps = sb("ln_eps", [P, 1])
        n_eps = sb("n_eps", [P, 1])
        ln_qs = sb("ln_qs", [P, 1])
        w_rows = x1[0:2 * NH, :, :, :].rearrange("p a t e -> p (a t e)")[:, 0:3 * E]
        f_val, f_mag, f_tmp = (dec[:, i, :] for i in range(3))

        bank = [es.enter_context(nc.psum_tensor(f"bank{i}", [P, 512], f32)) for i in range(8)]
        turn_ps = bank[0:2]
        gate_ps, arg_ps, qk_ps = bank[2], bank[3], bank[4]
        work_ps = bank[5:7]
        y_ps = bank[7]
        part_ps = gate_ps[:, 0:S]
        rows_ps = gate_ps[0:2 * R, S:2 * S]
        facs_ps = gate_ps[:, S:S + 4 * R]
        zt_ps = y_ps[:, :].bitcast(bf16)

        x_in = [sem(f"x_in{r}") for r in range(RING)]
        c_in = [sem(f"c_in{r}") for r in range(RING)]
        stored = sem("stored")
        gate_w_in, scales_in, consts_in = sem("gate_w_in"), sem("scales_in"), sem("consts_in")
        pool_set, gate_w_turned, dve_set = sem("pool_set"), sem("gate_w_turned"), sem("dve_set")
        ffn_w_set = sem("ffn_w_set")
        v_norm = Stage(sem("v_norm"), "bn0 bn1 mv0 mv1 nb")
        a_norm = Stage(sem("a_norm"), "log r q0 q1")
        t_turn = Stage(sem("t_turn"), "r0 r1 r2 r3 gates")
        a_turn = Stage(sem("a_turn"), "r0 r1 r2 r3 gates")
        t_scan = Stage(sem("t_scan"), "rows turned", GROUP)
        v_scan = Stage(sem("v_scan"), "z neg abs ncs a m ex0 ex1 ex2 negm p1 rest p2 p2b p3", GROUP)
        a_scan = Stage(sem("a_scan"), "exp log ex facs", GROUP)
        v_val = Stage(sem("v_val"), "sum mean")
        p_val = Stage(sem("p_val"), "val0 val1")
        t_first = Stage(sem("t_first"), "arg0")
        t_attn = Stage(sem("t_attn"), "arg1 qk0 arg2 qk1 st arg3 qk2 pv1 pv0 qk3 in0 in1 pv2")
        t_last = Stage(sem("t_last"), "pv3")
        a_first = Stage(sem("a_first"), "exp0")
        a_attn = Stage(sem("a_attn"), "exp1 exp2 st exp3 g0 g1")
        p_attn = Stage(sem("p_attn"), "mask0 mask1 kw mask2 mask3")
        v_attn = Stage(sem("v_attn"), "c0 c1 c2 in0 in1 c3 g2")
        v_last = Stage(sem("v_last"), "g3")
        a_mix = Stage(sem("a_mix"), "sq n2 hlog hr log r z0 z1")
        v_mix = Stage(sem("v_mix"), "n0 n ss v hn x1 bn0 bn1 mv0 mv1 nb")
        p_mix = Stage(sem("p_mix"), "hw0 hw1 x1")
        t_ffn = Stage(sem("t_ffn"), "zt y0 y1")
        a_ffn = Stage(sem("a_ffn"), "zq y0 y1")
        v_ffn = Stage(sem("v_ffn"), "yb")
        v_wide = Stage(sem("v_wide"), " ".join(f"{step}{i}" for i in range(WIDE_PIECES) for step in
                                               ROUNDING.split()))
        p_ffn = Stage(sem("p_ffn"), "out0 out1")

        block = es.enter_context(nc.Block())

        def slots(eng, slot, *mode):
            for k in range(-6, RING):
                slot(Batch(0, k), *mode)
            with eng.Fori(1, B // RING - 1) as it:
                for k in range(RING):
                    slot(Batch(it, k), *mode)
            for k in range(RING + 3):
                slot(Batch(B // RING - 1, k), *mode)

        def slots_by_range(eng, slot):
            with eng.If(eng.value_load(wide[0:1, 0:1].bitcast(i32)) > 0):
                slots(eng, slot, True)
            with eng.Else():
                slots(eng, slot, False)

        def scans(b):
            return b.k % GROUP == 0 and b.exists(B)

        def heads(ap):
            return ap.rearrange("p (h d) -> p h d", d=DH)

        N_CONSTS = 16 * (5 + 2 * GROUP)
        N_FFN_W_SET = len(ROUNDING.split()) * C
        N_POOL_SET, N_DVE_SET = 5, 12

        @block.sync
        def _(sp):
            def rows_of(t, b):
                return t[bass.ds(b.index, 1), :, :].rearrange("o (t p) e -> p (o t) e", p=P)

            def load(b):
                r = b.k % RING
                if b.follows(RING):
                    sp.wait_ge(v_mix.sem, v_mix.at(b - RING, "bn1"))
                sp.dma_start(x_sb[:, r, :, :], rows_of(x, b)).then_inc(x_in[r], 16)
                if b.follows(RING):
                    sp.wait_ge(p_attn.sem, p_attn.at(b - RING, "kw"))
                sp.dma_start(c_sb[:, r, :, :], rows_of(ctx, b)).then_inc(c_in[r], 16)

            sp.dma_start(ident[:, :], c_ident).then_inc(gate_w_in, 16)
            sp.dma_start(w_rows[0:NH, :], igate_w).then_inc(gate_w_in, 16)
            sp.dma_start(w_rows[NH:2 * NH, :], fgate_w).then_inc(gate_w_in, 16)
            for col, s in ((0, s_in), (1, s_k)):
                sp.dma_start(sc[:, col:col + 1], s.partition_broadcast(P)).then_inc(scales_in, 16)
            sp.dma_start(hsel_f[:, :], c_hsel).then_inc(consts_in, 16)
            sp.dma_start(gsel[:, :, :], c_gsel).then_inc(consts_in, 16)
            load(Batch(0, 0))
            for j in range(GROUP):
                for dst, src in ((b_i, igate_b), (b_f, fgate_b)):
                    sp.dma_start(dst[j * NH:(j + 1) * NH, :],
                                 src.rearrange("(h o) -> h o", o=1)).then_inc(consts_in, 16)
            sp.dma_start(w_ffn[:, :, :], ffn_w.rearrange("(c p) f -> p c f", p=P)).then_inc(consts_in, 16)
            sp.dma_start(w_out[:, :], out_w.partition_broadcast(P)).then_inc(consts_in, 16)
            sp.dma_start(b_ffn[:, :], bias.partition_broadcast(P)).then_inc(consts_in, 16)

            def slot(m):
                if (m - 3).exists(B):
                    sp.wait_ge(p_ffn.sem, p_ffn.at(m - 3, "out1"))
                    sp.dma_start(rows_of(out, m - 3), o_sb[:, :, :]).then_inc(stored, 16)
                if (m + 7).exists(B):
                    load(m + 7)

            slots(sp, slot)
            sp.wait_ge(stored, 16 * B)

        @block.tensor
        def _(pe):
            mm, turn = nc.tensor.matmul, nc.tensor.transpose

            pe.wait_ge(gate_w_in, 48)
            for i in range(3 * C):
                last = turn(gate_ps[:, i * 2 * NH:(i + 1) * 2 * NH], w_rows[:, i * P:(i + 1) * P],
                            ident[0:2 * NH, 0:2 * NH])
            last.then_inc(gate_w_turned, 1)
            pe.wait_ge(dve_set, N_DVE_SET)
            pe.wait_ge(pool_set, N_POOL_SET)
            pe.wait_ge(consts_in, N_CONSTS)

            def turn_round(b, i):
                if i == 0:
                    pe.wait_ge(a_norm.sem, a_norm.at(b, "q1"))
                if i == 2:
                    pe.wait_ge(c_in[b.k % RING], b.count(16, 16, RING))
                if i >= 2:
                    pe.wait_ge(a_turn.sem, a_turn.at(b, f"r{i - 2}"))
                elif b.follows(1):
                    pe.wait_ge(a_turn.sem, a_turn.at(b - 1, f"r{i + 2}"))
                for c in range(2):
                    for t in range(T):
                        chunk = slice((2 * (i % 2) + c) * P, (2 * (i % 2) + c + 1) * P)
                        src = q_nat[:, t, chunk] if i < 2 else c_sb[:, b.k % RING, t, chunk]
                        last = turn(turn_ps[i % 2][:, (T * c + t) * P:(T * c + t + 1) * P], src, ident[:, :])
                last.then_inc(t_turn.sem, 1)

            def gates(b):
                r = b.k % RING
                pe.wait_ge(a_turn.sem, a_turn.at(b, "r3"))
                if b.follows(1):
                    pe.wait_ge(a_turn.sem, a_turn.at(b - 1, "gates"))
                if b.k % GROUP == 0 and b.follows(GROUP):
                    pe.wait_ge(v_scan.sem, v_scan.at(b - GROUP, "a"))
                for w, src, first in ((w_x, qT, True), (w_c, kT, False)):
                    for c in range(C):
                        last = mm(part_ps[32 * c:32 * c + 32, :], w[:, c, :], src[:, r, c, :],
                                  start=first, stop=not first)
                last.then_inc(t_turn.sem, 1)

            def scan_rows(b):
                pe.wait_ge(a_turn.sem, a_turn.at(b + (GROUP - 1), "gates"))
                if b.follows(GROUP):
                    pe.wait_ge(a_scan.sem, a_scan.at(b - GROUP, "facs"))
                for j in range(GROUP):
                    last = mm(rows_ps, gsel[:, j, :], g_part[:, j, :], start=j == 0, stop=j == GROUP - 1)
                last.then_inc(t_scan.sem, 1)

            def scan_turned(b):
                for i in range(4):
                    last = turn(facs_ps[:, i * R:(i + 1) * R], ex[:, i * P:(i + 1) * P], ident[0:R, 0:R])
                last.then_inc(t_scan.sem, 1)

            def arg(b, q):
                t, u, j, g = q // U, q % U, b.k % GROUP, b.k // GROUP % 2
                row = j * NH + u
                if q == 0:
                    pe.wait_ge(v_scan.sem, v_scan.at(b, "p3"))
                if q == 1:
                    pe.wait_ge(a_first.sem, a_first.at(b, "exp0"))
                elif q:
                    pe.wait_ge(a_attn.sem, a_attn.at(b, f"exp{q - 1}"))
                elif b.follows(1):
                    pe.wait_ge(a_attn.sem, a_attn.at(b - 1, "exp3"))
                mm(arg_ps[:, :], split[:, g, t * P:(t + 1) * P], hsel[:, row:row + NH - 1:2].unsqueeze(2).broadcast_to([P, 4, P]),
                   start=True, stop=False)
                for h in range(4):
                    last = mm(arg_ps[:, h * P:(h + 1) * P], hsel[:, row + 2 * h:row + 2 * h + 1].broadcast_to([P, P]),
                              split[:, g, S + t * P:S + (t + 1) * P], start=False, stop=h == 3)
                last.then_inc((t_attn if q else t_first).sem, 1)

            def scores(b, q):
                t, u, r = q // U, q % U, b.k % RING
                if q:
                    pe.wait_ge(v_attn.sem, v_attn.at(b, f"c{q - 1}"))
                elif b.follows(1):
                    pe.wait_ge(v_attn.sem, v_attn.at(b - 1, "c3"))
                half = slice(DH * u, DH * u + DH)
                for c in range(C):
                    last = mm(qk_ps[:, c * P:(c + 1) * P], kT[half, r, c, t * P:(t + 1) * P],
                              qT[half, r, c, t * P:(t + 1) * P], start=True, stop=True)
                last.then_inc(t_attn.sem, 1)

            def states(b):
                pe.wait_ge(p_attn.sem, p_attn.at(b, "kw"))
                pe.wait_ge(p_val.sem, p_val.at(b, "val1"))
                if b.follows(1):
                    pe.wait_ge(v_attn.sem, v_attn.at(b - 1, "g2"))
                for pair in range(C):
                    for half in range(2):
                        h = 2 * pair + half
                        last = mm(work_ps[0][half * DH:(half + 1) * DH, pair * W:(pair + 1) * W],
                                  k_w[:, h * DH:(h + 1) * DH], val[:, b.k % 2, h, :], start=True, stop=True)
                last.then_inc(t_attn.sem, 1)

            def within(b, q):
                t, u = q // U, q % U
                pe.wait_ge(v_attn.sem, v_attn.at(b, ("c0", "c1", "in0", "c3")[q]))
                if q == 0:
                    pe.wait_ge(a_attn.sem, a_attn.at(b, "st"))
                elif q == 1 and b.follows(1):
                    pe.wait_ge(v_last.sem, v_last.at(b - 1, "g3"))
                for h in range(4):
                    for half in range(2):
                        rows = slice(half * P // 2, (half + 1) * P // 2)
                        last = mm(work_ps[u][rows, h * W:(h + 1) * W],
                                  dec[:, q, h * P + rows.start:h * P + rows.stop],
                                  val[:, b.k % 2, t * NH + 2 * h + u, :], start=True, stop=True)
                last.then_inc((t_attn if q < 3 else t_last).sem, 1)

            def across(b, u):
                pe.wait_ge(a_attn.sem, a_attn.at(b, f"g{u}"))
                for i in range(2):
                    last = mm(work_ps[u][:, i * 2 * W:(i + 1) * 2 * W], qT[:, b.k % RING, 2 * u + i, P:2 * P],
                              state[:, 2 * u + i, :], start=True, stop=True)
                last.then_inc(t_attn.sem, 1)

            def ffn_turn(b):
                pe.wait_ge(a_mix.sem, a_mix.at(b, "z1"))
                if b.follows(1):
                    pe.wait_ge(a_ffn.sem, a_ffn.at(b - 1, "y1"))
                for c in range(C):
                    for t in range(T):
                        last = turn(zt_ps[:, c * S + t * P:c * S + (t + 1) * P],
                                    z_bf[:, t, c * P:(c + 1) * P], ident_bf[:, :])
                last.then_inc(t_ffn.sem, 1)

            def ffn(b, t, wide_z):
                if t == 0 and not b.follows(1):
                    pe.wait_ge(ffn_w_set, N_FFN_W_SET)
                if wide_z and t == 0:
                    pe.wait_ge(v_wide.sem, v_wide.at(b, f"out{WIDE_PIECES - 1}"))
                for c in range(C):
                    last = mm(y_ps[:, :], (zq_wide if wide_z else zq)[:, c, t * P:(t + 1) * P],
                              w_ffn[:, c, :], start=c == 0, stop=c == C - 1)
                last.then_inc(t_ffn.sem, 1)

            def slot(m, wide_z):
                turning, opening, attending, closing, feeding = ((m + d).exists(B) for d in (5, 1, 0, -1, -2))
                if turning:
                    turn_round(m + 5, 0)
                if attending:
                    arg(m, 1)
                if turning:
                    turn_round(m + 5, 1)
                    turn_round(m + 5, 2)
                if attending:
                    scores(m, 0)
                if closing:
                    within(m - 1, 3)
                if turning:
                    turn_round(m + 5, 3)
                if attending:
                    arg(m, 2)
                    scores(m, 1)
                if feeding:
                    ffn_turn(m - 2)
                if turning:
                    gates(m + 5)
                if attending:
                    states(m)
                    arg(m, 3)
                if scans(m + 2):
                    scan_rows(m + 2)
                if feeding:
                    pe.wait_ge(a_ffn.sem, a_ffn.at(m - 2, "zq"))
                if attending:
                    scores(m, 2)
                    within(m, 1)
                if feeding:
                    ffn(m - 2, 0, wide_z)
                if attending:
                    within(m, 0)
                    scores(m, 3)
                if feeding:
                    pe.wait_ge(a_ffn.sem, a_ffn.at(m - 2, "y0"))
                if attending:
                    across(m, 0)
                    across(m, 1)
                if feeding:
                    ffn(m - 2, 1, wide_z)
                if scans(m + 1):
                    pe.wait_ge(a_scan.sem, a_scan.at(m + 1, "ex"))
                if opening:
                    arg(m + 1, 0)
                if scans(m + 1):
                    scan_turned(m + 1)
                if attending:
                    within(m, 2)

            slots_by_range(pe, slot)

        @block.scalar
        def _(act):
            af = nc.scalar.activation
            nc.scalar.preload_act_table_set("natural_log_exp_and_others")
            act.wait_ge(dve_set, N_DVE_SET)
            act.wait_ge(pool_set, N_POOL_SET)

            def turned(b, i):
                act.wait_ge(t_turn.sem, t_turn.at(b, f"r{i}"))
                dst = (qT if i < 2 else kT)[:, b.k % RING, 2 * (i % 2):2 * (i % 2) + 2, :]
                af(dst.rearrange("p c s -> p (c s)"), turn_ps[i % 2][:, :], ACT.Copy).then_inc(a_turn.sem, 1)

            def gates(b):
                act.wait_ge(t_turn.sem, t_turn.at(b, "gates"))
                af(g_part[:, b.k % GROUP, :], part_ps, ACT.Copy).then_inc(a_turn.sem, 1)

            def decay(b, q):
                if q == 0 and not b.follows(1):
                    act.wait_ge(ffn_w_set, N_FFN_W_SET)
                if q == 0:
                    act.wait_ge(t_first.sem, t_first.at(b, "arg0"))
                else:
                    act.wait_ge(t_attn.sem, t_attn.at(b, f"arg{q}"))
                af(dec[:, q, :], arg_ps[:, :], ACT.Exp).then_inc((a_attn if q else a_first).sem, 1)

            def keep_states(b):
                act.wait_ge(t_attn.sem, t_attn.at(b, "st"))
                src = work_ps[0][:, 0:C * W].rearrange("p (i w) -> p i w", i=C)
                af(state[0:DH, :, 0:W], src[0:DH, :, :], ACT.Copy)
                af(state[DH:P, :, W:2 * W], src[DH:P, :, :], ACT.Copy).then_inc(a_attn.sem, 1)

            def keep_tile0(b, u):
                act.wait_ge(t_attn.sem, t_attn.at(b, f"pv{u}"))
                if b.follows(2):
                    act.wait_ge(v_mix.sem, v_mix.at(b - 2, "hn"))
                af(g_sb[:, b.k % 2, u:NH:2, :], work_ps[u][:, 0:4 * W].rearrange("p (h w) -> p h w", w=W),
                   ACT.Copy).then_inc(a_attn.sem, 1)

            def norm_rstd(b):
                act.wait_ge(v_norm.sem, v_norm.at(b, "mv1"))
                af(log1[:, :], mv1[:, :, 1], ACT.Ln, bias=ln_eps[:, :]).then_inc(a_norm.sem, 1)
                act.wait_ge(a_norm.sem, a_norm.at(b, "log"))
                af(r1[:, :], log1[:, :], ACT.Exp, scale=-0.5, bias=ln_qs[:, :]).then_inc(a_norm.sem, 1)

            def norm_apply(b, t):
                if t == 0:
                    act.wait_ge(v_norm.sem, v_norm.at(b, "nb"))
                    if b.follows(1):
                        act.wait_ge(t_turn.sem, t_turn.at(b - 1, "r1"))
                af(q_nat[:, t, :], x_sb[:, b.k % RING, t, :], ACT.Identity, bias=nb1[:, t:t + 1],
                   scale=r1[:, t:t + 1]).then_inc(a_norm.sem, 1)

            def scan_softplus(b):
                act.wait_ge(v_scan.sem, v_scan.at(b, "abs"))
                af(z_abs[:, :], z_abs[:, :], ACT.Exp, scale=-1.0).then_inc(a_scan.sem, 1)
                act.wait_ge(a_scan.sem, a_scan.at(b, "exp"))
                af(z_abs[:, :], z_abs[:, :], ACT.Ln, bias=1.0).then_inc(a_scan.sem, 1)

            def scan_exps(b):
                act.wait_ge(v_scan.sem, v_scan.at(b, "ex2"))
                af(ex[:, :], ex[:, :], ACT.Exp).then_inc(a_scan.sem, 1)

            def scan_facs(b):
                act.wait_ge(t_scan.sem, t_scan.at(b, "turned"))
                af(facs[:, b.k // GROUP % 2, :, :].rearrange("p k r -> p (k r)"), facs_ps,
                   ACT.Copy).then_inc(a_scan.sem, 1)

            def squares(b):
                act.wait_ge(v_last.sem, v_last.at(b, "g3"))
                act.wait_ge(a_attn.sem, a_attn.at(b, "g1"))
                if b.follows(2):
                    act.wait_ge(p_ffn.sem, p_ffn.at(b - 2, "out1"))
                af(x1[:, b.k % 2, :, :].rearrange("p t (h d) -> p (t h) d", d=DH),
                   g_sb[:, b.k % 2, :, 0:DH], ACT.Square).then_inc(a_mix.sem, 1)

            def normaliser_square(b):
                act.wait_ge(v_mix.sem, v_mix.at(b, "n"))
                af(h_n2[:, :], h_n[:, :, :].rearrange("p t h -> p (t h)"), ACT.Square,
                   bias=n_eps[:, :]).then_inc(a_mix.sem, 1)

            def head_rstd(b):
                act.wait_ge(v_mix.sem, v_mix.at(b, "v"))
                af(h_log[:, :], h_v[:, :], ACT.Ln, scale=1.0 / DH).then_inc(a_mix.sem, 1)
                act.wait_ge(a_mix.sem, a_mix.at(b, "hlog"))
                af(h_r[:, :], h_log[:, :], ACT.Exp, scale=-0.5).then_inc(a_mix.sem, 1)

            def mix_rstd(b):
                act.wait_ge(v_mix.sem, v_mix.at(b, "mv1"))
                af(log2[:, :], mv2[:, :, 1], ACT.Ln, bias=ln_eps[:, :]).then_inc(a_mix.sem, 1)
                act.wait_ge(a_mix.sem, a_mix.at(b, "log"))
                af(r2[:, :], log2[:, :], ACT.Exp, scale=-0.5).then_inc(a_mix.sem, 1)

            def mix_apply(b, t):
                if t == 0:
                    act.wait_ge(v_mix.sem, v_mix.at(b, "nb"))
                    if b.follows(1):
                        act.wait_ge(t_ffn.sem, t_ffn.at(b - 1, "zt"))
                af(z_bf[:, t, :], x1[:, b.k % 2, t, :], ACT.Identity, bias=nb2[:, t:t + 1],
                   scale=r2[:, t:t + 1]).then_inc(a_mix.sem, 1)

            def quantise(b):
                af(zq[:, :, :].rearrange("p c s -> p (c s)"), zt_ps, ACT.Copy, scale=s_inv[:, 0:1],
                   saturate=False).then_inc(a_ffn.sem, 1)

            def dequantise(b, t):
                act.wait_ge(t_ffn.sem, t_ffn.at(b, f"y{t}"))
                if t == 0:
                    if b.follows(1):
                        act.wait_ge(p_ffn.sem, p_ffn.at(b - 1, "out1"))
                af(y_bf[:, t, :], y_ps[:, :], ACT.Copy, scale=s_out[:, :]).then_inc(a_ffn.sem, 1)

            def slot(m):
                norming, turning, opening, attending, mixing, feeding = (
                    (m + d).exists(B) for d in (6, 5, 1, 0, -1, -2))
                if turning:
                    turned(m + 5, 0)
                if attending:
                    decay(m, 1)
                if feeding:
                    mix_rstd(m - 2)
                if turning:
                    turned(m + 5, 1)
                if feeding:
                    mix_apply(m - 2, 0)
                    mix_apply(m - 2, 1)
                if turning:
                    turned(m + 5, 2)
                    turned(m + 5, 3)
                if attending:
                    decay(m, 2)
                if mixing:
                    squares(m - 1)
                if feeding:
                    act.wait_ge(t_ffn.sem, t_ffn.at(m - 2, "zt"))
                if mixing:
                    normaliser_square(m - 1)
                if feeding:
                    quantise(m - 2)
                if scans(m + 1):
                    scan_exps(m + 1)
                if turning:
                    gates(m + 5)
                if mixing:
                    head_rstd(m - 1)
                if norming:
                    norm_rstd(m + 6)
                if attending:
                    keep_states(m)
                    decay(m, 3)
                if scans(m + 2):
                    scan_softplus(m + 2)
                if norming:
                    norm_apply(m + 6, 0)
                if feeding:
                    dequantise(m - 2, 0)
                if attending:
                    keep_tile0(m, 0)
                    keep_tile0(m, 1)
                if norming:
                    norm_apply(m + 6, 1)
                if feeding:
                    dequantise(m - 2, 1)
                if opening:
                    decay(m + 1, 0)
                if scans(m + 1):
                    scan_facs(m + 1)

            slots(act, slot)

        @block.vector
        def _(dve):
            ve = nc.vector
            tt, ts, stt = ve.tensor_tensor, ve.tensor_scalar, ve.scalar_tensor_tensor
            done = [0]

            def setup(ins):
                done[0] += 1
                ins.then_inc(dve_set, 1)
                dve.wait_ge(dve_set, done[0])

            dve.wait_ge(pool_set, N_POOL_SET)
            setup(ve.memset(ln_eps[:, :], LN_EPS))
            setup(ve.memset(n_eps[:, :], EPS))
            setup(ve.memset(ln_qs[:, :], math.log(Q_SCALE)))
            dve.wait_ge(gate_w_in, 48)
            setup(ve.tensor_copy(ident_bf[:, :], ident[:, :]))
            dve.wait_ge(gate_w_turned, 1)
            turned = gate_ps[:, 0:3 * C * 2 * NH].rearrange("p (k c g) -> p k c g", k=3, c=C)
            setup(ts(w_x[:, :, 0:2 * NH], turned[:, 0, :, :], 1.0 / Q_SCALE, None, ALU.mult))
            setup(ve.tensor_copy(w_c[:, :, 0:2 * NH], turned[:, 1, :, :]))
            setup(tt(w_c[:, :, 0:2 * NH], turned[:, 2, :, :], w_c[:, :, 0:2 * NH], ALU.add))
            dve.wait_ge(scales_in, 32)
            setup(ve.reciprocal(s_inv[:, :], sc[:, :]))
            setup(tt(s_out[:, :], sc[:, 0:1], sc[:, 1:2], ALU.mult))
            setup(stt(s_abs[:, :], sc[:, 0:1], -1.0, sc[:, 0:1], ALU.mult, ALU.max))
            setup(ts(wide[:, :], s_abs[:, :], 22.7 / 240, None, ALU.is_lt))
            dve.wait_ge(consts_in, N_CONSTS)
            setup(ve.tensor_copy(hsel[:, :], hsel_f[:, :]))
            assert done[0] == N_DVE_SET

            def round_e4m3fn(out, src, scale, val, mag, tmp, step):
                step(ts(val, src, scale, None, ALU.mult))
                step(ts(mag.bitcast(i32), val.bitcast(i32), 0x7F800000, None, ALU.bitwise_and))
                step(ts(mag, mag, 2.0 ** -6, 1.5 * 2.0 ** 20, ALU.max, ALU.mult))
                step(tt(tmp, val, mag, ALU.add))
                step(tt(val, tmp, mag, ALU.subtract))
                step(stt(tmp, val, -1.0, val, ALU.mult, ALU.max))
                step(ts(tmp, tmp, 448.0, 3e38, ALU.is_gt, ALU.mult))
                step(ts(mag, tmp, 3e38, None, ALU.mult))
                step(stt(out, mag, 0.0, val, ALU.mult, ALU.add))

            def ffn_weights(c):
                steps = [0]

                def step(ins):
                    steps[0] += 1
                    ins.then_inc(ffn_w_set, 1)
                    dve.wait_ge(ffn_w_set, c * len(ROUNDING.split()) + steps[0])

                round_e4m3fn(w_ffn[:, c, :], w_ffn[:, c, :], s_inv[:, 1:2], f_val, f_mag, f_tmp, step)

            def norm_stats(b):
                r = b.k % RING
                dve.wait_ge(x_in[r], b.count(16, 16, RING))
                for t in range(T):
                    ve.bn_stats(bn1[:, t, :], x_sb[:, r, t, :]).then_inc(v_norm.sem, 1)

            def norm_moments(b):
                for t in range(T):
                    ve.bn_aggr(mv1[:, t, :], bn1[:, t, :]).then_inc(v_norm.sem, 1)

            def norm_scale(b):
                dve.wait_ge(a_norm.sem, a_norm.at(b, "r"))
                stt(nb1[:, :], mv1[:, :, 0], -1.0, r1[:, :], ALU.mult, ALU.mult).then_inc(v_norm.sem, 1)

            def value_sums(b):
                r = b.k % RING
                dve.wait_ge(c_in[r], b.count(16, 16, RING))
                ve.tensor_reduce(v_sum[:, :], c_sb[:, r, :, :].rearrange("p t (h d) -> p (t h) d", d=DH),
                                 AX.X, ALU.add).then_inc(v_val.sem, 1)

            def value_means(b):
                dve.wait_ge(v_val.sem, v_val.at(b, "sum"))
                if b.follows(1):
                    dve.wait_ge(p_val.sem, p_val.at(b - 1, "val1"))
                ts(v_mean[:, :], v_sum[:, :], 1.0 / DH, None, ALU.mult).then_inc(v_val.sem, 1)

            def matrix(b, q):
                dve.wait_ge(t_attn.sem, t_attn.at(b, f"qk{q}"))
                dve.wait_ge(p_attn.sem, p_attn.at(b, f"mask{q}"))
                tt(dec[:, q, :], qk_ps[:, :], dec[:, q, :], ALU.mult).then_inc(v_attn.sem, 1)

            def carried(b, u):
                row, g = b.k % GROUP * NH + 4 * u, b.k // GROUP % 2
                dve.wait_ge(t_attn.sem, t_attn.at(b, f"in{u}"))
                tt(carry[:, 4 * u:4 * u + 4, :], work_ps[u][:, 0:4 * W].rearrange("p (h w) -> p h w", w=W),
                   facs[:, g, 2, row:row + 4].unsqueeze(2).broadcast_to([P, 4, W]),
                   ALU.mult).then_inc(v_attn.sem, 1)

            def keep_tile1(b, u):
                if u == 0:
                    dve.wait_ge(t_attn.sem, t_attn.at(b, "pv2"))
                    dve.wait_ge(v_attn.sem, v_attn.at(b, "in1"))
                else:
                    dve.wait_ge(t_last.sem, t_last.at(b, "pv3"))
                tt(g_sb[:, b.k % 2, NH + u:2 * NH:2, :], work_ps[u][:, 0:4 * W].rearrange("p (h w) -> p h w", w=W),
                   carry[:, u:NH:2, :], ALU.add).then_inc((v_last if u else v_attn).sem, 1)

            def normaliser(b):
                dve.wait_ge(v_last.sem, v_last.at(b, "g3"))
                dve.wait_ge(a_attn.sem, a_attn.at(b, "g1"))
                row, g = b.k % GROUP * NH, b.k // GROUP % 2
                sums = g_sb[:, b.k % 2, :, DH].rearrange("p (t h) -> p t h", t=T)
                stt(h_n0[:, :, :], sums, -1.0, facs[:, g, 0:T, row:row + NH], ALU.mult,
                    ALU.max).then_inc(v_mix.sem, 1)
                dve.wait_ge(v_mix.sem, v_mix.at(b, "n0"))
                stt(h_n[:, :, :], h_n0[:, :, :], TOP, sums, ALU.min, ALU.max).then_inc(v_mix.sem, 1)

            def head_squares(b):
                dve.wait_ge(a_mix.sem, a_mix.at(b, "sq"))
                ve.tensor_reduce(g_ss[:, :], x1[:, b.k % 2, :, :].rearrange("p t (h d) -> p (t h) d", d=DH),
                                 AX.X, ALU.add).then_inc(v_mix.sem, 1)

            def head_var(b):
                dve.wait_ge(v_mix.sem, v_mix.at(b, "ss"))
                dve.wait_ge(a_mix.sem, a_mix.at(b, "n2"))
                stt(h_v[:, :], h_n2[:, :], LN_EPS * DH, g_ss[:, :], ALU.mult, ALU.add).then_inc(v_mix.sem, 1)

            def head_norm(b):
                dve.wait_ge(a_mix.sem, a_mix.at(b, "hr"))
                tt(x1[:, b.k % 2, :, :].rearrange("p t (h d) -> p (t h) d", d=DH), g_sb[:, b.k % 2, :, 0:DH],
                   h_r[:, :].unsqueeze(2).broadcast_to([P, T * NH, DH]), ALU.mult).then_inc(v_mix.sem, 1)

            def residual(b):
                dve.wait_ge(p_mix.sem, p_mix.at(b, "hw0"))
                tt(x1[:, b.k % 2, 0, :], x1[:, b.k % 2, 0, :], x_sb[:, b.k % RING, 0, :],
                   ALU.add).then_inc(v_mix.sem, 1)

            def mix_stats(b, t):
                if t == 0:
                    dve.wait_ge(v_mix.sem, v_mix.at(b, "x1"))
                else:
                    dve.wait_ge(p_mix.sem, p_mix.at(b, "x1"))
                ve.bn_stats(bn2[:, t, :], x1[:, b.k % 2, t, :]).then_inc(v_mix.sem, 1)

            def mix_moments(b):
                for t in range(T):
                    ve.bn_aggr(mv2[:, t, :], bn2[:, t, :]).then_inc(v_mix.sem, 1)

            def mix_scale(b):
                dve.wait_ge(a_mix.sem, a_mix.at(b, "r"))
                stt(nb2[:, :], mv2[:, :, 0], -1.0, r2[:, :], ALU.mult, ALU.mult).then_inc(v_mix.sem, 1)

            def quantise_wide(b):
                pieces = zq_wide.rearrange("p c s -> p (c s)").rearrange("p (i n) -> p i n", i=WIDE_PIECES)
                turned = zt_ps.rearrange("p (i n) -> p i n", i=WIDE_PIECES)
                steps = [0]

                def step(ins):
                    steps[0] += 1
                    ins.then_inc(v_wide.sem, 1)
                    if steps[0] < len(v_wide.steps):
                        dve.wait_ge(v_wide.sem, b.count(len(v_wide.steps), steps[0]))

                dve.wait_ge(a_ffn.sem, a_ffn.at(b, "zq"))
                for i in range(WIDE_PIECES):
                    round_e4m3fn(pieces[:, i, :], turned[:, i, :], s_inv[:, 0:1], wide_val,
                                 wide_mag, wide_tmp, step)

            def add_bias(b):
                dve.wait_ge(a_ffn.sem, a_ffn.at(b, "y1"))
                tt(y_bf[:, :, :], y_bf[:, :, :], b_ffn[:, :].unsqueeze(1).broadcast_to([P, T, F]),
                   ALU.add).then_inc(v_ffn.sem, 1)

            def scan_gate(b):
                dve.wait_ge(t_scan.sem, t_scan.at(b, "rows"))
                ts(z_f, rows_ps[R:2 * R, :], b_f[:, :], None, ALU.add).then_inc(v_scan.sem, 1)
                dve.wait_ge(v_scan.sem, v_scan.at(b, "z"))
                ts(z_neg, z_f, -1.0, 0.0, ALU.mult, ALU.max).then_inc(v_scan.sem, 1)
                stt(z_abs[:, :], z_f, -1.0, z_f, ALU.mult, ALU.max).then_inc(v_scan.sem, 1)

            def scan_sums(b):
                dve.wait_ge(a_scan.sem, a_scan.at(b, "log"))
                ve.tensor_tensor_scan(ncs[:, :], z_abs[:, :], z_neg, 0.0, ALU.add,
                                      ALU.add).then_inc(v_scan.sem, 1)
                dve.wait_ge(v_scan.sem, v_scan.at(b, "ncs"))
                stt(am[:, 0:S], rows_ps[0:R, :], b_i[:, :], ncs[:, :], ALU.add, ALU.add).then_inc(v_scan.sem, 1)
                dve.wait_ge(v_scan.sem, v_scan.at(b, "a"))
                ve.tensor_tensor_scan(mx[:, :], am[:, 0:S], am[:, 0:S], -3.0e38, ALU.max,
                                      ALU.max).then_inc(v_scan.sem, 1)
                dve.wait_ge(v_scan.sem, v_scan.at(b, "m"))
                tt(ex[:, 0:S], ncs[:, :], mx[:, :], ALU.subtract).then_inc(v_scan.sem, 1)
                ts(ex[:, S:S + P], mx[:, P:S], -1.0, mx[:, P - 1:P], ALU.mult, ALU.add).then_inc(v_scan.sem, 1)
                ts(ex[:, S + P:2 * S], am[:, 0:P], mx[:, P - 1:P], None, ALU.subtract).then_inc(v_scan.sem, 1)

            def scan_split(b):
                g = b.k // GROUP % 2
                ts(am[:, S:2 * S], mx[:, :], -1.0, None, ALU.mult).then_inc(v_scan.sem, 1)
                dve.wait_ge(v_scan.sem, v_scan.at(b, "negm"))
                ve.tensor_copy(split[0:R, g, :], am[:, :]).then_inc(v_scan.sem, 1)
                dve.wait_ge(v_scan.sem, v_scan.at(b, "p1"))
                tt(rest, am[:, :], split[0:R, g, :], ALU.subtract).then_inc(v_scan.sem, 1)

            def scan_split_rest(b):
                g = b.k // GROUP % 2
                dve.wait_ge(v_scan.sem, v_scan.at(b, "rest"))
                ve.tensor_copy(part2[:, :], rest).then_inc(v_scan.sem, 1)
                dve.wait_ge(v_scan.sem, v_scan.at(b, "p2"))
                ve.tensor_copy(split[R:2 * R, g, :], part2[:, :]).then_inc(v_scan.sem, 1)
                tt(split[2 * R:3 * R, g, :], rest, part2[:, :], ALU.subtract).then_inc(v_scan.sem, 1)

            def slot(m, wide_z):
                norming, valuing, attending, mixing, feeding = (
                    (m + d).exists(B) for d in (6, 1, 0, -1, -2))
                if m.known and m.index in range(-6, -6 + C):
                    ffn_weights(m.index + 6)
                if feeding:
                    mix_scale(m - 2)
                if valuing:
                    value_sums(m + 1)
                if attending:
                    matrix(m, 0)
                if mixing:
                    keep_tile1(m - 1, 1)
                if valuing:
                    value_means(m + 1)
                if norming:
                    norm_stats(m + 6)
                if mixing:
                    normaliser(m - 1)
                if attending:
                    matrix(m, 1)
                if feeding and wide_z:
                    quantise_wide(m - 2)
                if norming:
                    dve.wait_ge(v_norm.sem, v_norm.at(m + 6, "bn1"))
                if mixing:
                    head_squares(m - 1)
                if norming:
                    norm_moments(m + 6)
                if mixing:
                    head_var(m - 1)
                if scans(m + 1):
                    scan_split(m + 1)
                if mixing:
                    head_norm(m - 1)
                if scans(m + 2):
                    scan_gate(m + 2)
                if norming:
                    norm_scale(m + 6)
                if attending:
                    matrix(m, 2)
                if mixing:
                    residual(m - 1)
                if scans(m + 2):
                    scan_sums(m + 2)
                if scans(m + 1):
                    scan_split_rest(m + 1)
                if attending:
                    carried(m, 0)
                if mixing:
                    mix_stats(m - 1, 0)
                    mix_stats(m - 1, 1)
                if attending:
                    carried(m, 1)
                if feeding:
                    add_bias(m - 2)
                if mixing:
                    dve.wait_ge(v_mix.sem, v_mix.at(m - 1, "bn1"))
                if attending:
                    matrix(m, 3)
                if mixing:
                    mix_moments(m - 1)
                if attending:
                    keep_tile1(m, 0)

            slots_by_range(dve, slot)

        @block.gpsimd
        def _(pool):
            pl = nc.gpsimd
            pl.memset(val[:, :, :, DH:W], 1.0).then_inc(pool_set, 1)
            pl.memset(state[:, :, :], 0.0).then_inc(pool_set, 1)
            pl.memset(w_x[:, :, :], 0.0).then_inc(pool_set, 1)
            pl.memset(split[:, :, :], 0.0).then_inc(pool_set, 1)
            pl.memset(w_c[:, :, :], 0.0).then_inc(pool_set, 1)
            pool.wait_ge(consts_in, N_CONSTS)

            def weigh_keys(b):
                row, g = b.k % GROUP * NH, b.k // GROUP % 2
                pool.wait_ge(a_scan.sem, a_scan.at(b, "facs"))
                pool.wait_ge(c_in[b.k % RING], b.count(16, 16, RING))
                if b.follows(1):
                    pool.wait_ge(t_attn.sem, t_attn.at(b - 1, "st"))
                pl.tensor_tensor(heads(k_w[:, :]), heads(c_sb[:, b.k % RING, 0, :]),
                                 facs[:, g, 3, row:row + NH].unsqueeze(2).broadcast_to([P, NH, DH]),
                                 ALU.mult).then_inc(p_attn.sem, 1)

            def mask(b, q):
                pl.affine_select(out=dec[:, q, :], in_=dec[:, q, :], compare_op=ALU.is_ge, fill=0.0, base=0,
                                 pattern=[[0, 4], [1, P]], channel_multiplier=-1).then_inc(p_attn.sem, 1)

            def scale_heads(b, t):
                if t == 0:
                    pool.wait_ge(v_mix.sem, v_mix.at(b, "hn"))
                h = x1[:, b.k % 2, t, :]
                pl.tensor_tensor(h, h, w_out[:, :], ALU.mult).then_inc(p_mix.sem, 1)

            def residual(b):
                pool.wait_ge(p_mix.sem, p_mix.at(b, "hw1"))
                pl.tensor_tensor(x1[:, b.k % 2, 1, :], x1[:, b.k % 2, 1, :], x_sb[:, b.k % RING, 1, :],
                                 ALU.add).then_inc(p_mix.sem, 1)

            def wait_for_means(b):
                pool.wait_ge(v_val.sem, v_val.at(b, "mean"))
                if b.follows(2):
                    pool.wait_ge(t_last.sem, t_last.at(b - 2, "pv3"))

            def centre_values(b, t):
                pl.tensor_tensor(val[:, b.k % 2, t * NH:(t + 1) * NH, 0:DH], heads(c_sb[:, b.k % RING, t, :]),
                                 v_mean[:, t * NH:(t + 1) * NH].unsqueeze(2).broadcast_to([P, NH, DH]),
                                 ALU.subtract).then_inc(p_val.sem, 1)

            def output(b, t):
                if t == 0:
                    pool.wait_ge(v_ffn.sem, v_ffn.at(b, "yb"))
                    if b.follows(1):
                        pool.wait_ge(stored, b.count(16, 0))
                pl.tensor_tensor(o_sb[:, t, :], x1[:, b.k % 2, t, :], y_bf[:, t, :],
                                 ALU.add).then_inc(p_ffn.sem, 1)

            def slot(m):
                valuing, attending, mixing, leaving = ((m + d).exists(B) for d in (1, 0, -1, -3))
                if attending:
                    pool.wait_ge(a_first.sem, a_first.at(m, "exp0"))
                if leaving:
                    output(m - 3, 0)
                if attending:
                    mask(m, 0)
                    pool.wait_ge(a_attn.sem, a_attn.at(m, "exp1"))
                if leaving:
                    output(m - 3, 1)
                if attending:
                    mask(m, 1)
                    weigh_keys(m)
                if valuing:
                    wait_for_means(m + 1)
                if attending:
                    pool.wait_ge(a_attn.sem, a_attn.at(m, "exp2"))
                if valuing:
                    centre_values(m + 1, 1)
                if attending:
                    mask(m, 2)
                if mixing:
                    scale_heads(m - 1, 0)
                if attending:
                    pool.wait_ge(a_attn.sem, a_attn.at(m, "exp3"))
                if mixing:
                    scale_heads(m - 1, 1)
                    residual(m - 1)
                if attending:
                    mask(m, 3)
                if valuing:
                    centre_values(m + 1, 0)

            slots(pool, slot)


def shape_constants(n_heads):
    import numpy as np
    rows = GROUP * n_heads
    ident = np.eye(P, dtype=np.float32)
    gsel = np.zeros((P, GROUP, 2 * rows), np.float32)
    for chunk in range(P // 32):
        for j in range(GROUP):
            for h in range(n_heads):
                gsel[32 * chunk + h, j, j * n_heads + h] = 1
                gsel[32 * chunk + n_heads + h, j, rows + j * n_heads + h] = 1
    hsel = np.zeros((P, rows), np.float32)
    for part in range(3):
        for row in range(rows):
            hsel[part * rows + row, row] = 1
    return {"c_ident": ident, "c_gsel": gsel, "c_hsel": hsel}


INPUTS = ["x", "ctx_1024", "L0_xattn_igate_w", "L0_xattn_igate_b", "L0_xattn_fgate_w", "L0_xattn_fgate_b",
          "L0_xattn_out_w", "L0_ffn_kernel", "L0_ffn_input_scale", "L0_ffn_kernel_scale", "L0_ffn_bias"]


def kernel(**inputs):
    import numpy as np
    import concourse.bacc as bacc
    from concourse.bass_utils import run_bass_kernel_spmd

    nc = bacc.Bacc("TRN2", target_bir_lowering=False, num_devices=1)
    given = {name: np.ascontiguousarray(inputs[name]) for name in INPUTS}
    given.update(shape_constants(given["L0_xattn_igate_b"].shape[0]))
    arrays, args = {}, []
    for name, a in given.items():
        arrays[f"in_{name}"] = a
        args.append(nc.dram_tensor(f"in_{name}", a.shape, mybir.dt.from_np(a.dtype), kind="ExternalInput").ap())
    args.append(nc.dram_tensor("out_0", given["x"].shape, mybir.dt.float32, kind="ExternalOutput").ap())
    build_kernel(nc, *args)
    r = run_bass_kernel_spmd(nc, [arrays], core_ids=[0])
    return r.results[0]["out_0"]
```
